# Optimizing a Trainium2 kernel written in Bass

```python
import numpy as np
import jax
import jax.numpy as jnp

def _softmax(x, axis=-1):
    return jax.nn.softmax(x, axis=axis)

def _gelu(x):
    return jax.nn.gelu(x, approximate=True)

def _silu(x):
    return jax.nn.silu(x)

def _sigmoid(x):
    return jax.nn.sigmoid(x)

def _layernorm(x, axis=-1, eps=1e-05):
    m = jnp.mean(x, axis=axis, keepdims=True)
    v = jnp.var(x, axis=axis, keepdims=True)
    return (x - m) / jnp.sqrt(v + eps)

def _scatter_add(tgt, idx, src, axis=0):
    return tgt.at[idx].add(src)

def _segment_sum(src, seg, n):
    return jax.ops.segment_sum(src, seg, n)
kernel_name = 'mk_xattn_seq_d4_seqx_r8_170d8e'

def setup_inputs(seed: int=0):
    np.random.seed(seed)
    _w = jnp.asarray

    def _rec_inputs():
        import jax
        import jax.numpy as jnp
        _rk = jax.random.key(seed)
        x = -0.0001177 + 0.9999 * jax.random.normal(jax.random.fold_in(_rk, 1), (32, 56, 160), jnp.float32)
        _lenS = 56 - jax.random.randint(jax.random.fold_in(_rk, 7), (32,), 0, max(1, 56 // 4) + 1, jnp.int32)
        _lenS2 = 1500 - jax.random.randint(jax.random.fold_in(_rk, 8), (32,), 0, max(1, 1500 // 4) + 1, jnp.int32)
        _ctx_768P = jax.random.normal(jax.random.fold_in(_rk, 11), (32, 16, 96), jnp.float32)
        _ctx_768c = jax.random.dirichlet(jax.random.fold_in(_rk, 511), 0.3 * jnp.ones((16,), jnp.float32), (32, 1500))
        _ctx_768t = jnp.einsum('bsk,bkd->bsd', _ctx_768c, _ctx_768P)
        _ctx_768t = _ctx_768t * jax.lax.rsqrt(jnp.mean(jnp.square(_ctx_768t)) + 1e-12) * 0.953939
        ctx_768 = 0.00217967 + 0.999525 * (_ctx_768t + 0.3 * jax.random.normal(jax.random.fold_in(_rk, 611), (32, 1500, 96), jnp.float32))
        return (x, ctx_768)
    x, ctx_768 = _rec_inputs()

    def _L0_xattn_setup():
        import jax, jax.numpy as jnp
        import numpy as np
        B, S, DM, DC = (16, 512, 160, 96)
        N_AOE, N_IMG, N_DELTA = (16, 16, 16)
        ANAT_GATE, DIS_GATE, DELTA_SCALE = (0.5, 0.5, 1.0)

        def _heads(x, h):
            b, s, d = x.shape
            return x.reshape(b, s, h, d // h).transpose(0, 2, 1, 3)

        def _attend(q, k, v, scale):
            scores = jnp.einsum('bhqd,bhkd->bhqk', q, k) * scale
            probs = jax.nn.softmax(scores, axis=-1)
            return jnp.einsum('bhqk,bhkd->bhqd', probs, v)
        key = jax.random.key(seed)
        ks = jax.random.split(key, 9)

        def lin(k, fan_in, fan_out):
            return jax.random.normal(k, (fan_in, fan_out), jnp.float32) / np.sqrt(fan_in)
        return {'hidden_states': jax.random.normal(ks[0], (B, S, DM), jnp.float32), 'encoder_hidden_states': jax.random.normal(ks[1], (B, N_AOE + N_IMG + N_DELTA, DC), jnp.float32), 'w_q': lin(ks[2], DM, DM), 'w_k': lin(ks[3], DC, DM), 'w_v': lin(ks[4], DC, DM), 'w_k_dis': lin(ks[5], DC, DM), 'w_v_dis': lin(ks[6], DC, DM), 'w_out': lin(ks[7], DM, DM), 'b_out': jnp.zeros((DM,), jnp.float32), 'n_heads': 8}
    _L0_xattn_all = _L0_xattn_setup()
    _L0_xattn_in = {k: v for k, v in _L0_xattn_all.items() if k in ('w_q', 'w_k', 'w_v', 'w_k_dis', 'w_v_dis', 'w_out', 'b_out')}
    del _L0_xattn_all

    def _L1_xattn_setup():
        import jax, jax.numpy as jnp
        import numpy as np
        DIM, HEADS, DHEAD, CTX_DIM, DFF = (160, 20, 64, 96, 640)
        EPS = 1e-05
        SCALE = DHEAD ** (-0.5)

        def layer_norm(x, g, b):
            mu = jnp.mean(x, axis=-1, keepdims=True)
            var = jnp.mean(jnp.square(x - mu), axis=-1, keepdims=True)
            return (x - mu) * jax.lax.rsqrt(var + EPS) * g + b

        def cross_attention(x, ctx, wq, wk, wv, wo, bo):
            B, N, _ = x.shape
            M = ctx.shape[1]
            q = jnp.einsum('bne,ef->bnf', x, wq).reshape(B, N, HEADS, DHEAD).transpose(0, 2, 1, 3)
            k = jnp.einsum('bme,ef->bmf', ctx, wk).reshape(B, M, HEADS, DHEAD).transpose(0, 2, 1, 3)
            v = jnp.einsum('bme,ef->bmf', ctx, wv).reshape(B, M, HEADS, DHEAD).transpose(0, 2, 1, 3)
            scores = jnp.einsum('bhnd,bhmd->bhnm', q, k) * SCALE
            attn = jax.nn.softmax(scores, axis=-1)
            out = jnp.einsum('bhnm,bhmd->bhnd', attn, v)
            out = out.transpose(0, 2, 1, 3).reshape(B, N, HEADS * DHEAD)
            return jnp.einsum('bnf,fe->bne', out, wo) + bo

        def geglu_ff(x, w1, b1, w2, b2):
            h = jnp.einsum('bne,ef->bnf', x, w1) + b1
            a, gate = (h[..., :DFF], h[..., DFF:])
            h = a * jax.nn.gelu(gate)
            return jnp.einsum('bnf,fe->bne', h, w2) + b2

        def block_forward(x, context, g1, be1, wq1, wk1, wv1, wo1, bo1, g2, be2, wq2, wk2, wv2, wo2, bo2, g3, be3, w_ff1, b_ff1, w_ff2, b_ff2):
            x = cross_attention(layer_norm(x, g1, be1), layer_norm(x, g1, be1), wq1, wk1, wv1, wo1, bo1) + x
            x = cross_attention(layer_norm(x, g2, be2), context, wq2, wk2, wv2, wo2, bo2) + x
            return geglu_ff(layer_norm(x, g3, be3), w_ff1, b_ff1, w_ff2, b_ff2) + x
        key = jax.random.key(seed)
        ks = jax.random.split(key, 20)
        s = 0.02
        inner = HEADS * DHEAD
        return {'x': jax.random.normal(ks[0], (4, 128, DIM), jnp.float32), 'context': jax.random.normal(ks[1], (4, 77, CTX_DIM), jnp.float32), 'g1': jnp.ones((DIM,), jnp.float32), 'be1': jnp.zeros((DIM,), jnp.float32), 'wq1': jax.random.normal(ks[2], (DIM, inner), jnp.float32) * s, 'wk1': jax.random.normal(ks[3], (DIM, inner), jnp.float32) * s, 'wv1': jax.random.normal(ks[4], (DIM, inner), jnp.float32) * s, 'wo1': jax.random.normal(ks[5], (inner, DIM), jnp.float32) * s, 'bo1': jnp.zeros((DIM,), jnp.float32), 'g2': jnp.ones((DIM,), jnp.float32), 'be2': jnp.zeros((DIM,), jnp.float32), 'wq2': jax.random.normal(ks[6], (DIM, inner), jnp.float32) * s, 'wk2': jax.random.normal(ks[7], (CTX_DIM, inner), jnp.float32) * s, 'wv2': jax.random.normal(ks[8], (CTX_DIM, inner), jnp.float32) * s, 'wo2': jax.random.normal(ks[9], (inner, DIM), jnp.float32) * s, 'bo2': jnp.zeros((DIM,), jnp.float32), 'g3': jnp.ones((DIM,), jnp.float32), 'be3': jnp.zeros((DIM,), jnp.float32), 'w_ff1': jax.random.normal(ks[10], (DIM, 2 * DFF), jnp.float32) * s, 'b_ff1': jnp.zeros((2 * DFF,), jnp.float32), 'w_ff2': jax.random.normal(ks[11], (DFF, DIM), jnp.float32) * s, 'b_ff2': jnp.zeros((DIM,), jnp.float32)}
    _L1_xattn_all = _L1_xattn_setup()
    _L1_xattn_in = {k: v for k, v in _L1_xattn_all.items() if k in ('g1', 'be1', 'wq1', 'wk1', 'wv1', 'wo1', 'bo1', 'g2', 'be2', 'wq2', 'wk2', 'wv2', 'wo2', 'bo2', 'g3', 'be3', 'w_ff1', 'b_ff1', 'w_ff2', 'b_ff2')}
    del _L1_xattn_all

    def _L2_xattn_setup():
        import jax, jax.numpy as jnp
        import numpy as np
        HEADS = 8
        NUM_TOKENS = 4
        CROSS_ATTENTION_DIM = 96

        def _mha(q, k, v, heads=HEADS):
            B, Sq, H = q.shape
            Sk = k.shape[1]
            d = H // heads
            qh = q.reshape(B, Sq, heads, d).transpose(0, 2, 1, 3)
            kh = k.reshape(B, Sk, heads, d).transpose(0, 2, 1, 3)
            vh = v.reshape(B, Sk, heads, d).transpose(0, 2, 1, 3)
            scores = jnp.einsum('bhqd,bhkd->bhqk', qh, kh) * jnp.asarray(d, q.dtype) ** (-0.5)
            probs = jax.nn.softmax(scores, axis=-1)
            out = jnp.einsum('bhqk,bhkd->bhqd', probs, vh)
            return out.transpose(0, 2, 1, 3).reshape(B, Sq, H)
        key = jax.random.key(seed)
        ks = jax.random.split(key, 10)
        B, S, H, CAD, T = (4, 128, 160, CROSS_ATTENTION_DIM, NUM_TOKENS)
        sc = 0.02
        return {'hidden_states': jax.random.normal(ks[0], (B, S, H), jnp.float32), 'encoder_hidden_states': jax.random.normal(ks[1], (B, 77 + T, CAD), jnp.float32), 'Wq': jax.random.normal(ks[2], (H, H), jnp.float32) * sc, 'Wk': jax.random.normal(ks[3], (CAD, H), jnp.float32) * sc, 'Wv': jax.random.normal(ks[4], (CAD, H), jnp.float32) * sc, 'Wq_ca': jax.random.normal(ks[5], (T, H), jnp.float32) * sc, 'Wk_ca': jax.random.normal(ks[6], (CAD, H), jnp.float32) * sc, 'Wv_ca': jax.random.normal(ks[7], (CAD, H), jnp.float32) * sc, 'Wout': jax.random.normal(ks[8], (H, H), jnp.float32) * sc, 'b_out': jnp.zeros((H,), jnp.float32)}
    _L2_xattn_all = _L2_xattn_setup()
    _L2_xattn_in = {k: v for k, v in _L2_xattn_all.items() if k in ('Wq', 'Wk', 'Wv', 'Wq_ca', 'Wk_ca', 'Wv_ca', 'Wout', 'b_out')}
    del _L2_xattn_all

    def _L3_xattn_setup():
        import jax, jax.numpy as jnp
        import numpy as np
        D = 160
        H = 20
        DH = D // H
        CTX = 96
        FF_IN = 4 * D
        EPS = 1e-05

        def _ln(x, g, b):
            m = jnp.mean(x, axis=-1, keepdims=True)
            v = jnp.mean(jnp.square(x - m), axis=-1, keepdims=True)
            return (x - m) * jax.lax.rsqrt(v + EPS) * g + b

        def _attn(x, ctx, wq, wk, wv, wo, bo, heads):
            b, n, _ = x.shape
            j = ctx.shape[1]
            dh = wq.shape[1] // heads
            scale = dh ** (-0.5)
            q = (x @ wq).reshape(b, n, heads, dh).transpose(0, 2, 1, 3)
            k = (ctx @ wk).reshape(b, j, heads, dh).transpose(0, 2, 1, 3)
            v = (ctx @ wv).reshape(b, j, heads, dh).transpose(0, 2, 1, 3)
            sim = jnp.einsum('bhid,bhjd->bhij', q, k) * scale
            a = jax.nn.softmax(sim, axis=-1)
            out = jnp.einsum('bhij,bhjd->bhid', a, v)
            out = out.transpose(0, 2, 1, 3).reshape(b, n, heads * dh)
            return out @ wo + bo
        key = jax.random.key(seed)
        ks = jax.random.split(key, 24)
        r = lambda k, shp, s: jax.random.normal(k, shp, dtype=jnp.float32) * s
        d = {'x': r(ks[0], (8, 128, D), 1.0), 'context': r(ks[1], (8, 77, CTX), 1.0), 'heads': H, 'n1_g': jnp.ones((D,), jnp.float32), 'n1_b': jnp.zeros((D,), jnp.float32), 'q1': r(ks[2], (D, D), D ** (-0.5)), 'k1': r(ks[3], (D, D), D ** (-0.5)), 'v1': r(ks[4], (D, D), D ** (-0.5)), 'o1_w': r(ks[5], (D, D), D ** (-0.5)), 'o1_b': jnp.zeros((D,), jnp.float32), 'n2_g': jnp.ones((D,), jnp.float32), 'n2_b': jnp.zeros((D,), jnp.float32), 'q2': r(ks[6], (D, D), D ** (-0.5)), 'k2': r(ks[7], (CTX, D), CTX ** (-0.5)), 'v2': r(ks[8], (CTX, D), CTX ** (-0.5)), 'o2_w': r(ks[9], (D, D), D ** (-0.5)), 'o2_b': jnp.zeros((D,), jnp.float32), 'n3_g': jnp.ones((D,), jnp.float32), 'n3_b': jnp.zeros((D,), jnp.float32), 'ff_w1': r(ks[10], (D, 2 * FF_IN), D ** (-0.5)), 'ff_b1': jnp.zeros((2 * FF_IN,), jnp.float32), 'ff_w2': r(ks[11], (FF_IN, D), FF_IN ** (-0.5)), 'ff_b2': jnp.zeros((D,), jnp.float32)}
        return d
    _L3_xattn_all = _L3_xattn_setup()
    _L3_xattn_in = {k: v for k, v in _L3_xattn_all.items() if k in ('n1_g', 'n1_b', 'q1', 'k1', 'v1', 'o1_w', 'o1_b', 'n2_g', 'n2_b', 'q2', 'k2', 'v2', 'o2_w', 'o2_b', 'n3_g', 'n3_b', 'ff_w1', 'ff_b1', 'ff_w2', 'ff_b2')}
    del _L3_xattn_all
    return {'x': x, 'ctx_768': ctx_768, 'L0_xattn_w_q': _L0_xattn_in['w_q'], 'L0_xattn_w_k': _L0_xattn_in['w_k'], 'L0_xattn_w_v': _L0_xattn_in['w_v'], 'L0_xattn_w_k_dis': _L0_xattn_in['w_k_dis'], 'L0_xattn_w_v_dis': _L0_xattn_in['w_v_dis'], 'L0_xattn_w_out': _L0_xattn_in['w_out'], 'L0_xattn_b_out': _L0_xattn_in['b_out'], 'L1_xattn_g1': _L1_xattn_in['g1'], 'L1_xattn_be1': _L1_xattn_in['be1'], 'L1_xattn_wq1': _L1_xattn_in['wq1'], 'L1_xattn_wk1': _L1_xattn_in['wk1'], 'L1_xattn_wv1': _L1_xattn_in['wv1'], 'L1_xattn_wo1': _L1_xattn_in['wo1'], 'L1_xattn_bo1': _L1_xattn_in['bo1'], 'L1_xattn_g2': _L1_xattn_in['g2'], 'L1_xattn_be2': _L1_xattn_in['be2'], 'L1_xattn_wq2': _L1_xattn_in['wq2'], 'L1_xattn_wk2': _L1_xattn_in['wk2'], 'L1_xattn_wv2': _L1_xattn_in['wv2'], 'L1_xattn_wo2': _L1_xattn_in['wo2'], 'L1_xattn_bo2': _L1_xattn_in['bo2'], 'L1_xattn_g3': _L1_xattn_in['g3'], 'L1_xattn_be3': _L1_xattn_in['be3'], 'L1_xattn_w_ff1': _L1_xattn_in['w_ff1'], 'L1_xattn_b_ff1': _L1_xattn_in['b_ff1'], 'L1_xattn_w_ff2': _L1_xattn_in['w_ff2'], 'L1_xattn_b_ff2': _L1_xattn_in['b_ff2'], 'L2_xattn_Wq': _L2_xattn_in['Wq'], 'L2_xattn_Wk': _L2_xattn_in['Wk'], 'L2_xattn_Wv': _L2_xattn_in['Wv'], 'L2_xattn_Wq_ca': _L2_xattn_in['Wq_ca'], 'L2_xattn_Wk_ca': _L2_xattn_in['Wk_ca'], 'L2_xattn_Wv_ca': _L2_xattn_in['Wv_ca'], 'L2_xattn_Wout': _L2_xattn_in['Wout'], 'L2_xattn_b_out': _L2_xattn_in['b_out'], 'L3_xattn_n1_g': _L3_xattn_in['n1_g'], 'L3_xattn_n1_b': _L3_xattn_in['n1_b'], 'L3_xattn_q1': _L3_xattn_in['q1'], 'L3_xattn_k1': _L3_xattn_in['k1'], 'L3_xattn_v1': _L3_xattn_in['v1'], 'L3_xattn_o1_w': _L3_xattn_in['o1_w'], 'L3_xattn_o1_b': _L3_xattn_in['o1_b'], 'L3_xattn_n2_g': _L3_xattn_in['n2_g'], 'L3_xattn_n2_b': _L3_xattn_in['n2_b'], 'L3_xattn_q2': _L3_xattn_in['q2'], 'L3_xattn_k2': _L3_xattn_in['k2'], 'L3_xattn_v2': _L3_xattn_in['v2'], 'L3_xattn_o2_w': _L3_xattn_in['o2_w'], 'L3_xattn_o2_b': _L3_xattn_in['o2_b'], 'L3_xattn_n3_g': _L3_xattn_in['n3_g'], 'L3_xattn_n3_b': _L3_xattn_in['n3_b'], 'L3_xattn_ff_w1': _L3_xattn_in['ff_w1'], 'L3_xattn_ff_b1': _L3_xattn_in['ff_b1'], 'L3_xattn_ff_w2': _L3_xattn_in['ff_w2'], 'L3_xattn_ff_b2': _L3_xattn_in['ff_b2']}

def reference(x, ctx_768, L0_xattn_w_q, L0_xattn_w_k, L0_xattn_w_v, L0_xattn_w_k_dis, L0_xattn_w_v_dis, L0_xattn_w_out, L0_xattn_b_out, L1_xattn_g1, L1_xattn_be1, L1_xattn_wq1, L1_xattn_wk1, L1_xattn_wv1, L1_xattn_wo1, L1_xattn_bo1, L1_xattn_g2, L1_xattn_be2, L1_xattn_wq2, L1_xattn_wk2, L1_xattn_wv2, L1_xattn_wo2, L1_xattn_bo2, L1_xattn_g3, L1_xattn_be3, L1_xattn_w_ff1, L1_xattn_b_ff1, L1_xattn_w_ff2, L1_xattn_b_ff2, L2_xattn_Wq, L2_xattn_Wk, L2_xattn_Wv, L2_xattn_Wq_ca, L2_xattn_Wk_ca, L2_xattn_Wv_ca, L2_xattn_Wout, L2_xattn_b_out, L3_xattn_n1_g, L3_xattn_n1_b, L3_xattn_q1, L3_xattn_k1, L3_xattn_v1, L3_xattn_o1_w, L3_xattn_o1_b, L3_xattn_n2_g, L3_xattn_n2_b, L3_xattn_q2, L3_xattn_k2, L3_xattn_v2, L3_xattn_o2_w, L3_xattn_o2_b, L3_xattn_n3_g, L3_xattn_n3_b, L3_xattn_ff_w1, L3_xattn_ff_b1, L3_xattn_ff_w2, L3_xattn_ff_b2):
    import jax
    import jax.numpy as jnp

    def _L0_xattn_ref(hidden_states, encoder_hidden_states, w_q, w_k, w_v, w_k_dis, w_v_dis, w_out, b_out, n_heads):
        import jax, jax.numpy as jnp
        import numpy as np
        B, S, DM, DC = (16, 512, 160, 96)
        N_AOE, N_IMG, N_DELTA = (16, 16, 16)
        ANAT_GATE, DIS_GATE, DELTA_SCALE = (0.5, 0.5, 1.0)

        def _heads(x, h):
            b, s, d = x.shape
            return x.reshape(b, s, h, d // h).transpose(0, 2, 1, 3)

        def _attend(q, k, v, scale):
            scores = jnp.einsum('bhqd,bhkd->bhqk', q, k) * scale
            probs = jax.nn.softmax(scores, axis=-1)
            return jnp.einsum('bhqk,bhkd->bhqd', probs, v)
        residual = hidden_states
        dh = DM // n_heads
        scale = 1.0 / np.sqrt(dh)
        dis_tok = encoder_hidden_states[:, :N_AOE, :]
        anat_tok = encoder_hidden_states[:, N_AOE:N_AOE + N_IMG, :]
        delta_tok = encoder_hidden_states[:, -N_DELTA:, :]
        q = _heads(hidden_states @ w_q, n_heads)
        z_anat = _attend(q, _heads(anat_tok @ w_k, n_heads), _heads(anat_tok @ w_v, n_heads), scale)
        z_dis = _attend(q, _heads(dis_tok @ w_k_dis, n_heads), _heads(dis_tok @ w_v_dis, n_heads), scale)
        z_delta = _attend(q, _heads(delta_tok @ w_k_dis, n_heads), _heads(delta_tok @ w_v_dis, n_heads), scale)
        z = ANAT_GATE * z_anat + DIS_GATE * z_dis + DELTA_SCALE * z_delta
        out = z.transpose(0, 2, 1, 3).reshape(hidden_states.shape[0], -1, DM)
        out = out @ w_out + b_out
        return out + residual

    def _L1_xattn_ref(x, context, g1, be1, wq1, wk1, wv1, wo1, bo1, g2, be2, wq2, wk2, wv2, wo2, bo2, g3, be3, w_ff1, b_ff1, w_ff2, b_ff2):
        import jax, jax.numpy as jnp
        import numpy as np
        DIM, HEADS, DHEAD, CTX_DIM, DFF = (160, 20, 64, 96, 640)
        EPS = 1e-05
        SCALE = DHEAD ** (-0.5)

        def layer_norm(x, g, b):
            mu = jnp.mean(x, axis=-1, keepdims=True)
            var = jnp.mean(jnp.square(x - mu), axis=-1, keepdims=True)
            return (x - mu) * jax.lax.rsqrt(var + EPS) * g + b

        def cross_attention(x, ctx, wq, wk, wv, wo, bo):
            B, N, _ = x.shape
            M = ctx.shape[1]
            q = jnp.einsum('bne,ef->bnf', x, wq).reshape(B, N, HEADS, DHEAD).transpose(0, 2, 1, 3)
            k = jnp.einsum('bme,ef->bmf', ctx, wk).reshape(B, M, HEADS, DHEAD).transpose(0, 2, 1, 3)
            v = jnp.einsum('bme,ef->bmf', ctx, wv).reshape(B, M, HEADS, DHEAD).transpose(0, 2, 1, 3)
            scores = jnp.einsum('bhnd,bhmd->bhnm', q, k) * SCALE
            attn = jax.nn.softmax(scores, axis=-1)
            out = jnp.einsum('bhnm,bhmd->bhnd', attn, v)
            out = out.transpose(0, 2, 1, 3).reshape(B, N, HEADS * DHEAD)
            return jnp.einsum('bnf,fe->bne', out, wo) + bo

        def geglu_ff(x, w1, b1, w2, b2):
            h = jnp.einsum('bne,ef->bnf', x, w1) + b1
            a, gate = (h[..., :DFF], h[..., DFF:])
            h = a * jax.nn.gelu(gate)
            return jnp.einsum('bnf,fe->bne', h, w2) + b2

        def block_forward(x, context, g1, be1, wq1, wk1, wv1, wo1, bo1, g2, be2, wq2, wk2, wv2, wo2, bo2, g3, be3, w_ff1, b_ff1, w_ff2, b_ff2):
            x = cross_attention(layer_norm(x, g1, be1), layer_norm(x, g1, be1), wq1, wk1, wv1, wo1, bo1) + x
            x = cross_attention(layer_norm(x, g2, be2), context, wq2, wk2, wv2, wo2, bo2) + x
            return geglu_ff(layer_norm(x, g3, be3), w_ff1, b_ff1, w_ff2, b_ff2) + x
        return block_forward(x, context, g1, be1, wq1, wk1, wv1, wo1, bo1, g2, be2, wq2, wk2, wv2, wo2, bo2, g3, be3, w_ff1, b_ff1, w_ff2, b_ff2)

    def _L2_xattn_ref(hidden_states, encoder_hidden_states, Wq, Wk, Wv, Wq_ca, Wk_ca, Wv_ca, Wout, b_out):
        import jax, jax.numpy as jnp
        import numpy as np
        HEADS = 8
        NUM_TOKENS = 4
        CROSS_ATTENTION_DIM = 96

        def _mha(q, k, v, heads=HEADS):
            B, Sq, H = q.shape
            Sk = k.shape[1]
            d = H // heads
            qh = q.reshape(B, Sq, heads, d).transpose(0, 2, 1, 3)
            kh = k.reshape(B, Sk, heads, d).transpose(0, 2, 1, 3)
            vh = v.reshape(B, Sk, heads, d).transpose(0, 2, 1, 3)
            scores = jnp.einsum('bhqd,bhkd->bhqk', qh, kh) * jnp.asarray(d, q.dtype) ** (-0.5)
            probs = jax.nn.softmax(scores, axis=-1)
            out = jnp.einsum('bhqk,bhkd->bhqd', probs, vh)
            return out.transpose(0, 2, 1, 3).reshape(B, Sq, H)
        residual = hidden_states
        unet_size = residual.shape[1]
        end_pos = encoder_hidden_states.shape[1] - NUM_TOKENS
        enc = encoder_hidden_states[:, :end_pos, :]
        ca = encoder_hidden_states[:, end_pos:, :]
        query = hidden_states @ Wq
        keyt = enc @ Wk
        valt = enc @ Wv
        hs = _mha(query, keyt, valt)
        ca_q1 = jnp.einsum('btc,th->bch', ca, Wq_ca)
        indices = np.linspace(0, CROSS_ATTENTION_DIM - 1, unet_size).astype(np.int64)
        ca_q1 = ca_q1[:, indices, :]
        ca_hs1 = _mha(ca_q1, residual, residual)
        ca_q2 = ca_hs1 @ Wq
        ca_k2 = ca @ Wk_ca
        ca_v2 = ca @ Wv_ca
        ca_hs2 = _mha(ca_q2, ca_k2, ca_v2)
        out = hs + ca_hs2
        out = out @ Wout + b_out
        out = out + residual
        return out

    def _L3_xattn_ref(x, context, heads, n1_g, n1_b, q1, k1, v1, o1_w, o1_b, n2_g, n2_b, q2, k2, v2, o2_w, o2_b, n3_g, n3_b, ff_w1, ff_b1, ff_w2, ff_b2):
        import jax, jax.numpy as jnp
        import numpy as np
        D = 160
        H = 20
        DH = D // H
        CTX = 96
        FF_IN = 4 * D
        EPS = 1e-05

        def _ln(x, g, b):
            m = jnp.mean(x, axis=-1, keepdims=True)
            v = jnp.mean(jnp.square(x - m), axis=-1, keepdims=True)
            return (x - m) * jax.lax.rsqrt(v + EPS) * g + b

        def _attn(x, ctx, wq, wk, wv, wo, bo, heads):
            b, n, _ = x.shape
            j = ctx.shape[1]
            dh = wq.shape[1] // heads
            scale = dh ** (-0.5)
            q = (x @ wq).reshape(b, n, heads, dh).transpose(0, 2, 1, 3)
            k = (ctx @ wk).reshape(b, j, heads, dh).transpose(0, 2, 1, 3)
            v = (ctx @ wv).reshape(b, j, heads, dh).transpose(0, 2, 1, 3)
            sim = jnp.einsum('bhid,bhjd->bhij', q, k) * scale
            a = jax.nn.softmax(sim, axis=-1)
            out = jnp.einsum('bhij,bhjd->bhid', a, v)
            out = out.transpose(0, 2, 1, 3).reshape(b, n, heads * dh)
            return out @ wo + bo
        h1 = _ln(x, n1_g, n1_b)
        x = _attn(h1, h1, q1, k1, v1, o1_w, o1_b, heads) + x
        h2 = _ln(x, n2_g, n2_b)
        x = _attn(h2, context, q2, k2, v2, o2_w, o2_b, heads) + x
        h3 = _ln(x, n3_g, n3_b)
        proj = h3 @ ff_w1 + ff_b1
        a, g = jnp.split(proj, 2, axis=-1)
        ff = a * jax.nn.gelu(g, approximate=False) @ ff_w2 + ff_b2
        return ff + x
    x = _L0_xattn_ref(x, ctx_768, L0_xattn_w_q, L0_xattn_w_k, L0_xattn_w_v, L0_xattn_w_k_dis, L0_xattn_w_v_dis, L0_xattn_w_out, L0_xattn_b_out, 8)
    x = _L1_xattn_ref(x, ctx_768, L1_xattn_g1, L1_xattn_be1, L1_xattn_wq1, L1_xattn_wk1, L1_xattn_wv1, L1_xattn_wo1, L1_xattn_bo1, L1_xattn_g2, L1_xattn_be2, L1_xattn_wq2, L1_xattn_wk2, L1_xattn_wv2, L1_xattn_wo2, L1_xattn_bo2, L1_xattn_g3, L1_xattn_be3, L1_xattn_w_ff1, L1_xattn_b_ff1, L1_xattn_w_ff2, L1_xattn_b_ff2)
    x = _L2_xattn_ref(x, ctx_768, L2_xattn_Wq, L2_xattn_Wk, L2_xattn_Wv, L2_xattn_Wq_ca, L2_xattn_Wk_ca, L2_xattn_Wv_ca, L2_xattn_Wout, L2_xattn_b_out)
    x = _L3_xattn_ref(x, ctx_768, 20, L3_xattn_n1_g, L3_xattn_n1_b, L3_xattn_q1, L3_xattn_k1, L3_xattn_v1, L3_xattn_o1_w, L3_xattn_o1_b, L3_xattn_n2_g, L3_xattn_n2_b, L3_xattn_q2, L3_xattn_k2, L3_xattn_v2, L3_xattn_o2_w, L3_xattn_o2_b, L3_xattn_n3_g, L3_xattn_n3_b, L3_xattn_ff_w1, L3_xattn_ff_b1, L3_xattn_ff_w2, L3_xattn_ff_b2)
    return x

_drawn_inputs = setup_inputs


def setup_inputs(seed=0):
    import zlib

    import numpy as np

    out = dict(_drawn_inputs(seed))
    spreads = {'L0_xattn_b_out': (0.0, 0.1),
     'L1_xattn_g1': (1.0, 0.6),
     'L1_xattn_be1': (0.0, 0.424),
     'L1_xattn_bo1': (0.0, 0.1),
     'L1_xattn_g2': (1.0, 0.6),
     'L1_xattn_be2': (0.0, 0.8),
     'L1_xattn_bo2': (0.0, 0.1),
     'L1_xattn_g3': (1.0, 0.6),
     'L1_xattn_be3': (0.0, 0.8),
     'L1_xattn_b_ff1': (0.0, 0.8),
     'L1_xattn_b_ff2': (0.0, 0.315),
     'L2_xattn_b_out': (0.0, 0.275),
     'L3_xattn_n1_g': (1.0, 0.2),
     'L3_xattn_n1_b': (0.0, 0.314),
     'L3_xattn_o1_b': (0.0, 0.297),
     'L3_xattn_n2_g': (1.0, 0.6),
     'L3_xattn_n2_b': (0.0, 0.602),
     'L3_xattn_o2_b': (0.0, 0.342),
     'L3_xattn_n3_g': (1.0, 0.2),
     'L3_xattn_n3_b': (0.0, 0.298),
     'L3_xattn_ff_b1': (0.0, 0.324),
     'L3_xattn_ff_b2': (0.0, 0.328)}
    factors = {'L1_xattn_wq1': 8.0,
     'L1_xattn_wk1': 8.0,
     'L1_xattn_wq2': 8.0,
     'L1_xattn_wk2': 8.0,
     'L1_xattn_w_ff1': 3.678,
     'L1_xattn_w_ff2': 3.583,
     'L2_xattn_Wq': 8.0,
     'L2_xattn_Wk': 8.0,
     'L2_xattn_Wv': 2.725,
     'L2_xattn_Wq_ca': 64.0,
     'L2_xattn_Wk_ca': 51.271,
     'L2_xattn_Wv_ca': 4.535}
    for name, (base, spread) in spreads.items():
        noise = np.random.default_rng([zlib.crc32(name.encode()), seed]).standard_normal(out[name].shape)
        drawn = base * np.exp(spread * noise) if base else spread * noise
        out[name] = jnp.asarray(drawn.astype(out[name].dtype))
    for name, factor in factors.items():
        out[name] = (out[name] * factor).astype(out[name].dtype)
    return out
```

```python
from contextlib import ExitStack

import numpy as np
import concourse.bass as bass
from concourse import mybir

F32 = mybir.dt.float32
F32R = mybir.dt.float32r
ACT = mybir.ActivationFunctionType
ALU = mybir.AluOpType
AX = mybir.AxisListType

B, T, D = 32, 56, 160
KEYS, DC = 1500, 96
PAIRS = B // 2
S = 64
NC = 12
KP = KEYS // NC
HF = D // 2
EPS = 1e-5
PIECE = 4 * KP
NPIECE = KEYS // PIECE
HEADS = (20, 8, 20)
DH = (64, 20, 8)
CROSS_KEYS = (KEYS, KEYS - 4, KEYS)
NCA = 4
FF = 640


def groups(heads):
    return [(h, min(8, heads - h)) for h in range(0, heads, 8)]


class Signal:

    def __init__(self, sem, name, counts, credit):
        self.sem, self.name, self.counts, self.credit = sem, name, counts, credit
        self.seen = {}

    def __call__(self, t, k):
        before = self.credit + PAIRS * sum(self.counts[:t.ph])
        return self.sem, t.it * self.counts[t.ph] + (before + k)

    def end(self, ph):
        return self.sem, self.credit + PAIRS * sum(self.counts[:ph + 1])


class At:

    def __init__(self, ph, it):
        self.ph, self.it = ph, it
        self.heads = HEADS[ph]
        self.groups = groups(self.heads)

    def __add__(self, n):
        return At(self.ph, self.it + n)


COUNTS = {
    "x_loaded": ((64, 16, 16), 0), "cs_loaded": ((96, 96, 0), 0), "cr_loaded": ((32, 32, 32), 0),
    "x_saved": ((16, 16, 32), 1),
    "x_taken": ((1, 1, 1), 1), "x_handed": ((1, 1, 1), 1),
    "in_psum": ((1, 1, 0), 0), "cst_ready": ((1, 1, 0), 1), "xt_ready": ((1, 1, 0), 0),
    "ln_stats": ((2, 0, 2), 0), "ln_mean": ((2, 0, 2), 0), "ln_var": ((2, 0, 2), 0), "ln_rstd": ((2, 0, 2), 0),
    "xn_ready": ((2, 0, 2), 0), "xn_psum": ((2, 0, 2), 0), "ht_ready": ((2, 0, 2), 0),
    "qkv_psum": ((5, 1, 1), 0), "q_ready": ((2, 2, 1), 0), "kb_ready": ((2, 1, 1), 0), "kb2_ready": ((1, 0, 0), 0),
    "vb_ready": ((3, 1, 1), 0), "vb2_ready": ((2, 0, 0), 0),
    "ca_psum": ((0, 2, 0), 0), "ca_ready": ((0, 1, 0), 0), "k2_ready": ((0, 1, 0), 0),
    "s_psum": ((2, 2, 1), 0), "s_max": ((2, 2, 1), 0), "s_sub": ((2, 2, 1), 0), "s_exp": ((2, 2, 1), 0),
    "s_sum": ((2, 2, 1), 0), "s_rec": ((3, 2, 1), 0), "p_ready": ((2, 2, 1), 0),
    "pt_psum": ((2, 2, 1), 0), "pt_ready": ((2, 2, 1), 0), "o_psum": ((2, 2, 1), 0), "o_ready": ((2, 2, 1), 0),
    "ot_psum": ((1, 2, 1), 0), "ot_ready": ((1, 2, 1), 0), "rm_psum": ((2, 1, 1), 0), "xm_ready": ((2, 1, 1), 0),
    "qt_psum": ((6, 2, 6), 0), "qh_ready": ((6, 2, 6), 0), "ql_ready": ((6, 2, 6), 0),
    "ctx_hi": ((2, 2, 2), 0), "ctx_lo": ((2, 2, 2), 1),
    "ct_psum": ((6, 6, 6), 1), "cth_ready": ((6, 6, 6), 0), "ctl_ready": ((6, 6, 6), 0),
    "mp_psum": ((60, 24, 60), 0), "mp_ready": ((60, 24, 60), 0), "mx_ready": ((2, 2, 2), 0),
    "mr_psum": ((2, 2, 2), 0), "mr_ready": ((2, 2, 2), 0),
    "sc_psum": ((72, 24, 72), 0), "exp_done": ((72, 24, 72), 2),     "pl_ready": ((72, 24, 72), 2), "pv_done": ((72, 24, 72), 36),
    "u_copied": ((6, 2, 6), 3),
    "sum_psum": ((2, 2, 2), 0), "rec_ready": ((2, 2, 2), 0), "diag_ready": ((2, 2, 2), 0),
    "rb_psum": ((2, 2, 2), 0), "ut_ready": ((2, 2, 2), 2),
    "rp_psum": ((2, 1, 2), 1), "xp_ready": ((2, 1, 2), 1),
    "lnf_stats": ((1, 0, 1), 0), "lnf_mean": ((1, 0, 1), 0), "lnf_var": ((1, 0, 1), 0), "lnf_rstd": ((1, 0, 1), 0),
    "xnf_ready": ((1, 0, 1), 0), "xnf_psum": ((1, 0, 1), 0), "hf_ready": ((1, 0, 1), 0),
    "f_psum": ((1, 0, 1), 0), "gelu_ready": ((1, 0, 1), 0), "ff_ready": ((1, 0, 1), 0),
}


class Idle:

    @staticmethod
    def nothing(t, b=0, last=False):
        return iter(())

    pre = queries = context = maxima = normalise = hand = post = nothing


def xattn_stack(nc, a, sel, hmask, hmask32, out):
    es = ExitStack()
    with es:
        def sb(name, shape, dt=F32):
            return es.enter_context(nc.sbuf_tensor(name, shape, dt))

        w_area = sb("w_area", [128, 7680])
        w_o = sb("w_o", [128, 1600])
        w_m = sb("w_m", [HF, 2, 20 * DC])
        w_n = sb("w_n", [DC, 20, D])
        w_ff = sb("w_ff", [128, 3360])
        w_s = sb("w_s", [128, 1280])
        gb = sb("gb", [HF, 2, 8])
        bff = sb("bff", [128, 10])
        ident = sb("ident", [128, 128])
        ones = sb("ones", [128, 128])
        selc = sb("selc", [DC, S])
        hm = sb("hm", [HF, 14])
        hm32 = sb("hm32", [32, D])
        neghalf = sb("neghalf", [128, 1])
        eps = sb("eps", [128, 1])
        count = sb("count", [128, 1])
        countF = sb("countF", [128, 1])
        ctx_raw = sb("ctx_raw", [KP, NC * DC])
        ctx_hi = sb("ctx_hi", [KP, 2, NC, DC + 1], F32R)
        ctx_lo = sb("ctx_lo", [KP, 2, NC, DC], F32R)
        ctxT_hi = sb("ctxT_hi", [DC + 1, 2, KEYS], F32R)
        ctxT_lo = sb("ctxT_lo", [DC, 2, KEYS], F32R)
        q_hi = sb("q_hi", [DC + 1, 2, 20 * T], F32R)
        q_lo = sb("q_lo", [DC, 2, 20 * T], F32R)
        p32 = sb("p32", [KP, 2, 448])
        p_hi = sb("p_hi", [KP, 3, 448], F32R)
        p_lo = sb("p_lo", [KP, 3, 448], F32R)
        uT = sb("uT", [DC, 20, 2, S])
        mpiece = sb("mpiece", [112, 10, NPIECE])
        mx = sb("mx", [112, 10])
        srec = sb("srec", [112, 10])
        x_in = sb("x_in", [128, D])
        x_mid = sb("x_mid", [128, D])
        x_post = sb("x_post", [128, D])
        x_out = sb("x_out", [128, D])
        hF = sb("hF", [HF, 2, 2, S])
        xnF = sb("xnF", [128, D])
        statsF = sb("statsF", [128, 6])
        mvF = sb("mvF", [128, 2])
        veF = sb("veF", [128, 1])
        rstdF = sb("rstdF", [128, 1])
        cs = sb("cs", [128, DC])
        csT = sb("csT", [DC, 2, S])
        xT = sb("xT", [HF, 2, 2, S])
        hT = sb("hT", [HF, 2, 2, S])
        xn = sb("xn", [128, D])
        stats = sb("stats", [128, 6])
        mv = sb("mv", [128, 2])
        ve = sb("ve", [128, 1])
        rstd = sb("rstd", [128, 1])
        qo = sb("qo", [128, 10 * 128])
        kvb = sb("kvb", [128, 2 * 20 * 64])
        vb_s = sb("vb_s", [128, 320])
        sm = sb("sm", [128, 20 * S])
        pT = sb("pT", [128, 10 * 128])
        oz = sb("oz", [128, D])
        smx = sb("smx", [128, 24])
        ssum = sb("ssum", [128, 24])
        ca_r = sb("ca_r", [DC, 2, 8, NCA])

        ps_s = es.enter_context(nc.psum_tensor("ps_s", [128, 2, 512], F32))
        ps_u = es.enter_context(nc.psum_tensor("ps_u", [128, 3, 512], F32))
        ps_c = es.enter_context(nc.psum_tensor("ps_c", [128, 1536], F32))

        sg = {n: Signal(es.enter_context(nc.semaphore(n)), n, c, cr) for n, (c, cr) in COUNTS.items()}
        w_loaded = es.enter_context(nc.semaphore("w_loaded"))
        consts = es.enter_context(nc.semaphore("consts"))
        wt_psum = es.enter_context(nc.semaphore("wt_psum"))
        wt_ready = es.enter_context(nc.semaphore("wt_ready"))
        wp_psum = es.enter_context(nc.semaphore("wp_psum"))
        wp_ready = es.enter_context(nc.semaphore("wp_ready"))
        scratch = nc.dram_tensor("x_between", (PAIRS, 128, D), F32, kind="Internal").ap()

        fw1 = w_ff[0:HF, 0:2560].rearrange("p (a n) -> p a n", a=2)
        fw2 = w_ff[:, 2560:3360].rearrange("p (c n) -> p c n", c=5)
        wo_stage = w_ff[:, 0:3200].rearrange("p (h n) -> p h n", n=D)
        qo3 = qo[:, :].rearrange("p (j s) -> p j s", j=10)
        q_small = qo[0:HF, 1024:1280].rearrange("p (a b s) -> p a b s", a=2, b=2)
        p2 = sm[:, 1024:1056]
        k2b = hF[:, 0, :, :].rearrange("p b s -> p (b s)")[:, 0:64].rearrange("p (o b k) -> p o b k", o=2, b=2)
        u_sb = qo[0:DC + 1, 0:20 * T]
        diag = pT[0:112, 0:20 * T]
        caS = pT[0:NCA, 832:960]
        v2b = pT[0:32, 512:832].rearrange("p (b n) -> p b n", b=2)
        rows = w_s[DC:DC + 1, 0:4 * D]
        kb0 = qo[0:HF, 0:1024].rearrange("p (a b h s) -> p a b h s", a=2, b=2, h=4)
        kb1 = kvb[:, :].rearrange("p (b h s) -> p b h s", b=2, h=20)
        kb3 = kvb[0:HF, :].rearrange("p (a b h s) -> p a b h s", a=2, b=2, h=10)
        vb0 = vb_s[:, :].rearrange("p (b h d) -> p b h d", b=2, h=8)
        vb3 = vb_s[:, :].rearrange("p (b h d) -> p b h d", b=2, h=20)
        pT3 = pT[:, :].rearrange("p (k s) -> p k s", s=128)
        gT = pT[:, 0:640].rearrange("p (c s) -> p c s", c=5)
        smv = sm[:, :].rearrange("p (h s) -> p h s", s=S)

        def C(first, n_rows, bank, lo, n):
            return ps_c[first:first + n_rows, 512 * bank + lo:512 * bank + lo + n]

        def FC(c):
            return C(0, 128, *((2, 128 * c) if c < 4 else (1, 128) if c == 4 else (0, 128 * c - 640) if c < 9
                               else (1, 0)), 128)

        N_CONSTS = 12
        l0_wq = w_s[0:HF, 0:320].rearrange("p (a n) -> p a n", a=2)
        l0_wout = w_s[0:HF, 320:640].rearrange("p (a n) -> p a n", a=2)
        l0_wk = [w_s[0:DC, 640:800], w_s[0:DC, 800:960]]
        l0_wv = [w_s[0:DC, 960:1120], w_s[0:DC, 1120:1280]]
        l2_wqca = w_s[0:NCA, 640:800]
        l2_wkca = w_s[0:DC, 800:960]
        l2_wvca = w_s[0:DC, 960:1120]
        l1_w = [w_area[0:HF, 2560 * i:2560 * i + 2560].rearrange("p (a n) -> p a n", a=2) for i in range(3)]
        l3_w = [w_area[0:HF, 320 * i:320 * i + 320].rearrange("p (a n) -> p a n", a=2) for i in range(3)]
        l3_o = w_area[0:HF, 960:1280].rearrange("p (a n) -> p a n", a=2)
        l1_wo = w_o[:, :].rearrange("p (j n) -> p j n", j=10)

        FACTORS = (("L1_xattn_wq2", "L1_xattn_wk2", "L1_xattn_wv2", "L1_xattn_wo2"),
                   ("L2_xattn_Wq", "L2_xattn_Wk", "L2_xattn_Wv", "L2_xattn_Wout"),
                   ("L3_xattn_q2", "L3_xattn_k2", "L3_xattn_v2", "L3_xattn_o2_w"))

        def factor_views(ph):
            n = HEADS[ph] * DH[ph]
            fq = w_area[0:HF, 0:2 * n].rearrange("p (a n) -> p a n", a=2)
            fk = w_area[0:DC, 2560:2560 + n]
            fv = w_area[0:DC, 3840:3840 + n]
            fo = wo_stage[0:DH[ph], 0:HEADS[ph], :]
            return fq, fk, fv, fo

        def factorT(ph, h):
            return w_area[0:DH[ph], 5120 + 352 * (h % 4):5120 + 352 * (h % 4) + 352]

        LN = ((("L1_xattn_g1", "L1_xattn_be1"), ("L1_xattn_g2", "L1_xattn_be2"), ("L1_xattn_g3", "L1_xattn_be3")),
              (),
              (("L3_xattn_n1_g", "L3_xattn_n1_b"), ("L3_xattn_n2_g", "L3_xattn_n2_b"),
               ("L3_xattn_n3_g", "L3_xattn_n3_b")))
        BIAS = (("L0_xattn_b_out", "L1_xattn_bo1", "L1_xattn_bo2", "L1_xattn_b_ff2"),
                ("L2_xattn_b_out",),
                ("L3_xattn_o1_b", "L3_xattn_o2_b", "L3_xattn_ff_b2"))
        FFW = (("L1_xattn_w_ff1", "L1_xattn_b_ff1", "L1_xattn_w_ff2"), (),
               ("L3_xattn_ff_w1", "L3_xattn_ff_b1", "L3_xattn_ff_w2"))

        def halves(ap):
            return ap.rearrange("(a p) n -> p a n", a=2)

        def column(ap, n):
            return ap.rearrange("(a p o) -> p a o", a=n, o=1)

        def first_loads(ph):
            fq, fk, fv, fo = factor_views(ph)
            q, k, v, o = FACTORS[ph]
            return [(fq, halves(a[q])), (fk, a[k]), (fv, a[v]),
                    (fo, a[o].rearrange("(h d) n -> d h n", h=HEADS[ph]))]

        def other_loads(ph):
            r = [(rows[:, D * i:D * i + D], a[n].rearrange("(o n) -> o n", o=1)) for i, n in enumerate(BIAS[ph])]
            for i, (g, b) in enumerate(LN[ph]):
                r += [(gb[:, :, 2 * i:2 * i + 1], column(a[g], 2)), (gb[:, :, 2 * i + 1:2 * i + 2], column(a[b], 2))]
            if ph == 0:
                r += [(l0_wq, halves(a["L0_xattn_w_q"])), (l0_wout, halves(a["L0_xattn_w_out"])),
                      (l0_wk[0], a["L0_xattn_w_k_dis"]), (l0_wk[1], a["L0_xattn_w_k"]),
                      (l0_wv[0], a["L0_xattn_w_v_dis"]), (l0_wv[1], a["L0_xattn_w_v"]),
                      (selc[:, :], sel), (hm[:, :], hmask), (hm32[:, :], hmask32),
                      (l1_w[0], halves(a["L1_xattn_wq1"])), (l1_w[1], halves(a["L1_xattn_wk1"])),
                      (l1_w[2], halves(a["L1_xattn_wv1"])),
                      (l1_wo, a["L1_xattn_wo1"].rearrange("(j p) n -> p j n", j=10))]
            if ph == 1:
                r += [(l0_wq, halves(a["L2_xattn_Wq"])), (l0_wout, halves(a["L2_xattn_Wout"])),
                      (l2_wqca, a["L2_xattn_Wq_ca"]), (l2_wkca, a["L2_xattn_Wk_ca"]), (l2_wvca, a["L2_xattn_Wv_ca"])]
            if ph == 2:
                r += [(l3_w[0], halves(a["L3_xattn_q1"])), (l3_w[1], halves(a["L3_xattn_k1"])),
                      (l3_w[2], halves(a["L3_xattn_v1"])), (l3_o, halves(a["L3_xattn_o1_w"]))]
            if ph != 1:
                w1, b1, w2 = FFW[ph]
                r += [(fw1, halves(a[w1])), (fw2, a[w2].rearrange("(c p) n -> p c n", c=5)),
                      (bff[:, :].unsqueeze(2), a[b1].rearrange("(c p o) -> p c o", c=10, o=1))]
            return r

        FIRST = [len(first_loads(ph)) for ph in range(3)]
        OTHER = [len(other_loads(ph)) for ph in range(3)]

        def factors_loaded(ph):
            return w_loaded, 16 * (sum(FIRST[:ph]) + sum(OTHER[:ph]) + FIRST[ph])

        def weights_loaded(ph):
            return w_loaded, 16 * (sum(FIRST[:ph + 1]) + sum(OTHER[:ph + 1]))

        def products_before(ph):
            return sum(HEADS[:ph])

        now = {"ph": 0, "count": False}

        def got(name, t, k):
            return sg[name](t, k)

        def sig(name):
            if now["count"]:
                sg[name].seen[now["ph"]] = sg[name].seen.get(now["ph"], 0) + 1
            return sg[name].sem, 1

        def per(name, t):
            return sg[name].counts[t.ph]

        PRE = (40, 29, 20)
        POST = (11, 2, 11)
        CUT = (15, 13, 3)

        def schedule(eng, side, main):
            def part(step, length, weight, *args, **kw):
                return step(*args, **kw), length, weight

            def cut(steps, length, weight, last):
                pending = []

                def head():
                    number = next(steps, None)
                    while number is not None and number <= last:
                        yield number
                        number = next(steps, None)
                    pending.append(number)

                def tail():
                    number = pending[0]
                    while number is not None:
                        yield number - last
                        number = next(steps, None)

                return (head(), last, weight), (tail(), length - last, weight)

            def before(t, b):
                return [part(side.queries, 4, 1, t, b), part(side.context, 4, 2, t, b),
                        part(side.maxima, 3 * t.heads // 2 + 4, 1, t, b)]

            def weave(steps, parts):
                total = sum(length * weight for _, length, weight in parts)
                slots = 2 * NC * len(groups(HEADS[now["ph"]]))

                def labelled():
                    start = 0
                    for f, length, weight in parts:
                        for number in f:
                            yield start + weight * number
                        start += weight * length

                beside = labelled()
                due = next(beside, None)
                for n in steps:
                    if n:
                        while due is not None and due * slots <= total * n:
                            due = next(beside, None)
                while due is not None:
                    due = next(beside, None)

            def pair(t, first=False, last=False):
                parts = [] if first else [part(side.normalise, 7, 2, t + (-1), 1)]
                parts += before(t, 1)
                parts += [] if first else [part(side.post, POST[t.ph], 3, t + (-1))]
                parts += [part(side.hand, 1, 1, t)]
                if not last:
                    pre_a, pre_b = cut(*part(side.pre, PRE[t.ph], 3, t + 1), CUT[t.ph])
                    parts += [pre_a]
                weave(main(t, 0), parts)
                parts = [part(side.normalise, 7, 2, t, 0, last=last)]
                if not last:
                    parts += [pre_b] + before(t + 1, 0)
                weave(main(t, 1), parts)

            for ph in range(3):
                now.update(ph=ph)
                side.prologue(ph)
                t = At(ph, 0)
                weave(iter(()), [part(side.pre, PRE[ph], 3, t, first=True)] + before(t, 0))
                pair(t, first=True)
                with eng.Fori(1, PAIRS - 1) as it:
                    now.update(count=True)
                    pair(At(ph, it))
                    now.update(count=False)
                pair(At(ph, PAIRS - 1), last=True)
                t = At(ph, PAIRS - 1)
                weave(iter(()), [part(side.normalise, 7, 2, t, 1, last=True), part(side.post, POST[ph], 3, t, last=True)])

        block = es.enter_context(nc.Block())

        @block.sync
        def _(sp):
            cr = a["ctx_768"].rearrange("(i b) (p c) d -> i b p (c d)", b=2, c=NC)
            cx = a["ctx_768"].rearrange("(i b) k d -> i b k d", b=2)
            xv = a["x"].rearrange("(i b) t d -> i b t d", b=2)
            ov = out.rearrange("(i b) t d -> i b t d", b=2)

            def one(ap):
                return ap.rearrange("o p n -> (o p) n")

            for ph in range(3):
                if ph:
                    sp.wait_ge(*sg["xp_ready"].end(ph - 1))
                    sp.wait_ge(*sg["x_saved"].end(ph - 1))
                else:
                    sp.sem_inc(sg["x_saved"].sem, 1)
                    sp.wait_ge(consts, N_CONSTS)
                for dst, src in first_loads(ph):
                    sp.dma_start(dst, src).then_inc(w_loaded, 16)
                sp.wait_ge(wp_ready, products_before(ph + 1))
                with nc.allow_non_contiguous_dma(reason="gains and biases as columns, 640 B to 5 KB once a phase"):
                    for dst, src in other_loads(ph):
                        sp.dma_start(dst, src).then_inc(w_loaded, 16)

                def load_x(t):
                    i = bass.ds(t.it, 1)
                    sp.wait_ge(*got("x_taken", t, 0))
                    if ph < 2:
                        sp.wait_ge(*got("cst_ready", t, 0))
                    if ph == 0:
                        for b in range(2):
                            sp.dma_start(x_in[S * b:S * b + T, :], one(xv[i, b, :, :]))\
                                .then_inc(sg["x_loaded"].sem, 16)
                            sp.dma_start(x_in[S * b + T:S * b + S, :], one(xv[i, b, T - 8:T, :]))\
                                .then_inc(sg["x_loaded"].sem, 16)
                    else:
                        sp.dma_start(x_in[:, :], one(scratch[i, :, :])).then_inc(sg["x_loaded"].sem, 16)
                    if ph < 2:
                        for b in range(2):
                            for n, k in enumerate((0, KEYS - 16, 16)):
                                sp.dma_start(cs[S * b + 16 * n:S * b + 16 * n + 16, :], one(cx[i, b, k:k + 16, :]))\
                                    .then_inc(sg["cs_loaded"].sem, 16)

                def load_context(t, b):
                    sp.wait_ge(*got("ctx_lo", t, b))
                    sp.wait_ge(*got("ct_psum", t, 3 * b))
                    sp.dma_start(ctx_raw[:, :], one(cr[bass.ds(t.it, 1), b, :, :])).then_inc(sg["cr_loaded"].sem, 16)

                def save_x(t):
                    sp.wait_ge(*got("xp_ready", t, per("xp_ready", t)))
                    i = bass.ds(t.it, 1)
                    if ph < 2:
                        sp.dma_start(one(scratch[i, :, :]), x_out[:, :]).then_inc(sg["x_saved"].sem, 16)
                    else:
                        for b in range(2):
                            sp.dma_start(one(ov[i, b, :, :]), x_out[S * b:S * b + T, :])\
                                .then_inc(sg["x_saved"].sem, 16)

                def pair(t, first=False, last=False):
                    load_context(t, 1)
                    if not last:
                        load_x(t + 1)
                        load_context(t + 1, 0)
                    if not first:
                        save_x(t + (-1))

                load_x(At(ph, 0))
                load_context(At(ph, 0), 0)
                pair(At(ph, 0), first=True)
                with sp.Fori(1, PAIRS - 1) as it:
                    pair(At(ph, it))
                pair(At(ph, PAIRS - 1), last=True)
                save_x(At(ph, PAIRS - 1))
            sp.wait_ge(*sg["x_saved"].end(2))

        @block.tensor
        def _(pe):
            mm, tr = nc.tensor.matmul, nc.tensor.transpose

            def both(dst, lhsT, rhs, first=True, last=True):
                for i in range(2):
                    z = mm(dst, lhsT(i), rhs(i), start=(first and i == 0), stop=(last and i == 1))
                return z

            class side(Idle):
                @staticmethod
                def prologue(ph):
                    if ph == 0:
                        pe.sem_inc(sg["ct_psum"].sem, 1)
                        pe.sem_inc(sg["pv_done"].sem, 36)
                        pe.sem_inc(sg["rp_psum"].sem, 1)
                        pe.wait_ge(consts, N_CONSTS)
                    pe.wait_ge(*factors_loaded(ph))
                    fq, fk, fv, fo = factor_views(ph)
                    dh, n0 = DH[ph], products_before(ph)

                    def product(h):
                        f = factorT(ph, h)
                        pe.wait_ge(wt_ready, n0 + h + 1)
                        if n0 + h >= 2:
                            pe.wait_ge(wp_ready, n0 + h - 1)
                        for i in range(2):
                            mm(ps_u[0:HF, 1 + h % 2, DC * i:DC * i + DC], f[:, HF * i:HF * i + HF], f[:, 160:256],
                               start=True, stop=True)
                        mm(ps_u[0:DC, 1 + h % 2, 192:352], f[:, 256:352], fo[:, h, :],
                           start=True, stop=True).then_inc(wp_psum, 1)

                    for h in range(HEADS[ph]):
                        if n0 + h >= 2:
                            pe.wait_ge(wt_ready, n0 + h - 1)
                        for i in range(2):
                            tr(C(0, dh, h % 2, HF * i, HF), fq[:, i, dh * h:dh * h + dh], ident[0:HF, 0:HF])
                        tr(C(0, dh, h % 2, 160, DC), fk[:, dh * h:dh * h + dh], ident[0:DC, 0:DC])
                        tr(C(0, dh, h % 2, 256, DC), fv[:, dh * h:dh * h + dh], ident[0:DC, 0:DC])\
                            .then_inc(wt_psum, 1)
                        if h:
                            product(h - 1)
                    product(HEADS[ph] - 1)
                    pe.wait_ge(wp_ready, products_before(ph + 1))
                    pe.wait_ge(*weights_loaded(ph))

                @staticmethod
                def inputs(t):
                    pe.wait_ge(*got("cs_loaded", t, 96))
                    tr(C(0, DC, 0, 0, 128), cs[:, :], ident[:, :])
                    pe.wait_ge(*got("x_taken", t, 1))
                    for i in range(2):
                        z = tr(C(0, HF, 1, 128 * i, 128), x_mid[:, HF * i:HF * i + HF], ident[:, :])
                    z.then_inc(*sig("in_psum"))

                @staticmethod
                def norm(t, n, bank):
                    pe.wait_ge(*got("xn_ready", t, n + 1))
                    for i in range(2):
                        z = tr(C(0, HF, bank, 128 * i, 128), xn[:, HF * i:HF * i + HF], ident[:, :])
                    z.then_inc(*sig("xn_psum"))

                @staticmethod
                def probs_T(t, n, tiles, bank):
                    pe.wait_ge(*got("p_ready", t, n + 1))
                    for k in range(tiles):
                        z = tr(C(0, 128, bank, 128 * k, 128), sm[:, 128 * k:128 * k + 128], ident[:, :])
                    z.then_inc(*sig("pt_psum"))

                @staticmethod
                def out_slots(t, n, tiles, vb, d, bank):
                    pe.wait_ge(*got("pt_ready", t, n + 1))
                    for b in range(2):
                        for k in range(tiles):
                            z = mm(C(S * b, S, bank, 2 * d * k, 2 * d), pT3[:, k, S * b:S * b + S],
                                   vb[:, b, 2 * k:2 * k + 2, :], start=True, stop=True)
                    z.then_inc(*sig("o_psum"))

                @staticmethod
                def out_T(t, n, m, bank):
                    pe.wait_ge(*got("o_ready", t, n + 1))
                    for i in range(2):
                        z = tr(C(0, HF, bank, 128 * i, 128), oz[:, HF * i:HF * i + HF], ident[:, :])
                    z.then_inc(*sig("ot_psum"))

                @staticmethod
                def project(t, m, w, bias, bank):
                    pe.wait_ge(*got("ot_ready", t, m + 1))
                    r = C(0, 128, bank, 0, D)
                    mm(r, ones[DC:DC + 1, :], rows[:, D * bias:D * bias + D], start=True, stop=False)
                    both(r, lambda i: xT[:, i, :, :], lambda i: w[:, i, :], first=False).then_inc(*sig("rm_psum"))

                @staticmethod
                def resume(t):
                    pe.wait_ge(*got("ut_ready", t, -1))

                @staticmethod
                def pre(t, first=False):
                    yield 1
                    if not first:
                        pe.wait_ge(*got("mr_ready", t, 0))
                        pe.wait_ge(*got("xp_ready", t, -per("xp_ready", t)))
                    if t.ph == 0:
                        yield from side.pre_0(t)
                    elif t.ph == 1:
                        yield from side.pre_1(t)
                    else:
                        yield from side.pre_2(t)

                @staticmethod
                def pre_0(t):
                    yield 1
                    side.inputs(t)
                    yield 2
                    pe.wait_ge(*got("xt_ready", t, 1))
                    pe.wait_ge(*got("cst_ready", t, 1))
                    for o in range(2):
                        both(C(0, HF, 1, 128 * o, 128), lambda i: l0_wq[:, i, HF * o:HF * o + HF],
                             lambda i: xT[:, i, :, :])
                        kk = C(0, HF, 2, 128 * o, 128).rearrange("p (b w s) -> p b w s", b=2, w=2)
                        for w in range(2):
                            mm(kk[:, :, w, :], l0_wk[w][:, HF * o:HF * o + HF], csT[:, :, 32 * w:32 * w + 32],
                               start=True, stop=True)
                    for b in range(2):
                        for par in range(2):
                            for w in range(2):
                                vw = l0_wv[w].rearrange("p (h e d) -> p h e d", e=2, d=20)[:, :, par, :]
                                z = mm(C(S * par + 32 * w, 32, 0, 80 * b, 80), csT[:, b, 32 * w:32 * w + 32],
                                       vw, start=True, stop=True)
                    z.then_inc(*sig("qkv_psum"))
                    yield 4
                    pe.wait_ge(*got("q_ready", t, 1))
                    pe.wait_ge(*got("kb_ready", t, 1))
                    for b in range(2):
                        for o in range(2):
                            z = mm(C(S * b, S, 1, 256 * o, 256), q_small[:, o, b, :], kb0[:, o, b, :, :],
                                   start=True, stop=True)
                    z.then_inc(*sig("s_psum"))
                    yield 8
                    side.probs_T(t, 0, 4, 2)
                    yield 10
                    pe.wait_ge(*got("vb_ready", t, 1))
                    side.out_slots(t, 0, 4, vb0, 20, 0)
                    yield 12
                    side.out_T(t, 0, 0, 1)
                    yield 14
                    side.project(t, 0, l0_wout, 0, 2)
                    yield 16
                    side.resume(t)
                    side.norm(t, 0, 0)
                    for w in range(2):
                        for j in range(10):
                            if j % 5 == 0:
                                yield 18 + 3 * w + j // 5
                            if j == 0:
                                pe.wait_ge(*(got("q_ready", t, 2) if w else got("ht_ready", t, 1)))
                            z = both(C(0, 128, 0, 128 * j, 128), lambda i: l1_w[w][:, i, 128 * j:128 * j + 128],
                                     lambda i: hT[:, i, :, :])
                        z.then_inc(*sig("qkv_psum"))
                    for b in range(2):
                        yield 24 + b
                        if b == 0:
                            pe.wait_ge(*got("kb_ready", t, 2))
                            pe.wait_ge(*got("kb2_ready", t, 1))
                        for j in range(10):
                            z = mm(C(S * b, S, 0, 128 * j, 128), qo3[:, j, S * b:S * b + S],
                                   kb1[:, b, 2 * j:2 * j + 2, :], start=True, stop=True)
                    z.then_inc(*sig("s_psum"))
                    for b in range(2):
                        yield 27 + 3 * b
                        if b == 0:
                            pe.wait_ge(*got("s_sub", t, 2))
                        else:
                            pe.wait_ge(*got("vb_ready", t, 2))
                            pe.wait_ge(*got("vb2_ready", t, 1))
                        for par in range(2):
                            for f in range(2):
                                vw = l1_w[2].rearrange("p a (h e d) -> p a h e d", e=2, d=64)
                                z = both(C(S * par, S, f, 0, 320), lambda i: hT[:, i, b, :],
                                         lambda i: vw[:, i, 5 * f:5 * f + 5, par, :])
                        z.then_inc(*sig("qkv_psum"))
                    yield 32
                    pe.wait_ge(*got("vb_ready", t, 3))
                    pe.wait_ge(*got("vb2_ready", t, 2))
                    side.probs_T(t, 1, 10, 0)
                    for b in range(2):
                        yield 34 + b
                        if b == 0:
                            pe.wait_ge(*got("pt_ready", t, 2))
                        for k in range(10):
                            z = mm(C(0, 128, 0, 128 * k + S * b, S), kb1[:, b, 2 * k:2 * k + 2, :],
                                   pT3[:, k, S * b:S * b + S], start=True, stop=True)
                    z.then_inc(*sig("o_psum"))
                    yield 37
                    pe.wait_ge(*got("o_ready", t, 2))
                    r = C(0, 128, 0, 0, D)
                    mm(r, ones[DC:DC + 1, :], rows[:, D:2 * D], start=True, stop=False)
                    for j in range(10):
                        z = mm(r, qo3[:, j, :], l1_wo[:, j, :], start=False, stop=(j == 9))
                    z.then_inc(*sig("rm_psum"))
                    yield 39
                    side.norm(t, 1, 1)

                @staticmethod
                def pre_1(t):
                    yield 1
                    side.inputs(t)
                    yield 2
                    pe.wait_ge(*got("xt_ready", t, 1))
                    pe.wait_ge(*got("cst_ready", t, 1))
                    for b in range(2):
                        mm(C(0, NCA, 0, S * b, S), csT[:, b, 28:32], selc[:, :], start=True, stop=True)
                    for b in range(2):
                        for par in range(2):
                            z = mm(C(S * par, S, 2, 80 * b, 80), ident[:, S * b:S * b + S],
                                   x_mid[:, :].rearrange("p (h e d) -> p h e d", e=2, d=20)[:, :, par, :],
                                   start=True, stop=True)
                    z.then_inc(*sig("qkv_psum"))
                    yield 4
                    pe.wait_ge(*got("ca_ready", t, 1))
                    for o in range(2):
                        z = mm(C(0, HF, 1, 128 * o, 128), l2_wqca[:, HF * o:HF * o + HF], caS[:, :],
                               start=True, stop=True)
                    z.then_inc(*sig("ca_psum"))
                    yield 6
                    pe.wait_ge(*got("q_ready", t, 1))
                    pe.wait_ge(*got("kb_ready", t, 1))
                    for b in range(2):
                        for o in range(2):
                            z = mm(C(S * b, S, 0, 256 * o, 256), q_small[:, o, b, :], kb0[:, o, b, :, :],
                                   start=True, stop=True)
                    z.then_inc(*sig("s_psum"))
                    yield 10
                    pe.wait_ge(*got("vb_ready", t, 1))
                    side.probs_T(t, 0, 4, 2)
                    yield 12
                    side.out_slots(t, 0, 4, vb0, 20, 1)
                    yield 14
                    side.resume(t)
                    side.out_T(t, 0, 0, 0)
                    yield 16
                    pe.wait_ge(*got("ot_ready", t, 1))
                    for o in range(2):
                        both(C(0, HF, 1, 128 * o, 128), lambda i: l0_wq[:, i, HF * o:HF * o + HF],
                             lambda i: xT[:, i, :, :])
                        mm(C(0, HF, 2, 8 * o, 8), l2_wkca[:, HF * o:HF * o + HF], csT[:, :, 28:32],
                           start=True, stop=True)
                    for b in range(2):
                        z = mm(C(0, 32, 0, D * b, D), ca_r[:, b, :, :].rearrange("p h k -> p (h k)"),
                               l2_wvca, start=True, stop=True)
                    z.then_inc(*sig("ca_psum"))
                    yield 18
                    pe.wait_ge(*got("q_ready", t, 2))
                    pe.wait_ge(*got("k2_ready", t, 1))
                    for b in range(2):
                        for o in range(2):
                            z = mm(C(S * b, S, 2, 16 * o, 16), q_small[:, o, b, :], k2b[:, o, b, :],
                                   start=True, stop=True)
                    z.then_inc(*sig("s_psum"))
                    yield 22
                    pe.wait_ge(*got("p_ready", t, 2))
                    tr(C(0, 32, 0, 0, 128), p2[:, :], ident[:, :]).then_inc(*sig("pt_psum"))
                    yield 24
                    pe.wait_ge(*got("pt_ready", t, 2))
                    for b in range(2):
                        z = mm(C(S * b, S, 1, 0, D), pT[0:32, S * b:S * b + S], v2b[:, b, :], start=True, stop=True)
                    z.then_inc(*sig("o_psum"))
                    yield 26
                    side.out_T(t, 1, 1, 0)
                    yield 28
                    side.project(t, 1, l0_wout, 0, 1)

                @staticmethod
                def pre_2(t):
                    yield 2
                    side.norm(t, 0, 0)
                    yield 4
                    side.resume(t)
                    pe.wait_ge(*got("ht_ready", t, 1))
                    for o in range(2):
                        for w in range(2):
                            both(C(0, HF, 1 + w, 128 * o, 128), lambda i: l3_w[w][:, i, HF * o:HF * o + HF],
                                 lambda i: hT[:, i, :, :])
                    for b in range(2):
                        for par in range(2):
                            vw = l3_w[2].rearrange("p a (h e d) -> p a h e d", e=2, d=8)
                            z = both(C(S * par, S, 0, 80 * b, 80), lambda i: hT[:, i, b, :],
                                     lambda i: vw[:, i, :, par, :])
                    z.then_inc(*sig("qkv_psum"))
                    yield 7
                    pe.wait_ge(*got("q_ready", t, 1))
                    pe.wait_ge(*got("kb_ready", t, 1))
                    pe.wait_ge(*got("vb_ready", t, 1))
                    for b in range(2):
                        for o, h0, h1 in ((0, 0, 8), (0, 8, 10), (1, 0, 6), (1, 6, 10)):
                            z = mm(C(S * b, S, 0, 640 * o + S * h0, S * (h1 - h0)), q_small[:, o, b, :],
                                   kb3[:, o, b, h0:h1, :], start=True, stop=True)
                    z.then_inc(*sig("s_psum"))
                    yield 11
                    side.probs_T(t, 0, 10, 0)
                    yield 13
                    side.out_slots(t, 0, 10, vb3, 8, 0)
                    yield 15
                    side.out_T(t, 0, 0, 1)
                    yield 17
                    side.project(t, 0, l3_o, 0, 2)
                    yield 19
                    side.norm(t, 1, 0)

                @staticmethod
                def queries(t, b):
                    for g, (h0, n) in enumerate(t.groups):
                        yield 1 + g
                        if g == 0:
                            pe.wait_ge(*(got("ut_ready", t, 0) if b else got("xm_ready", t, per("xm_ready", t))))
                            if t.ph != 1:
                                pe.wait_ge(*got("ht_ready", t, 2))
                        for h in range(n):
                            z = both(C(0, DC, g, S * h, S), lambda i: w_m[:, i, DC * (h0 + h):DC * (h0 + h) + DC],
                                     lambda i: hT[:, i, b, :])
                        z.then_inc(*sig("qt_psum"))

                @staticmethod
                def context(t, b):
                    for r in range(NPIECE):
                        yield 1 + r
                        if r == 0:
                            pe.wait_ge(*got("cr_loaded", t, 16 * (b + 1)))
                            pe.wait_ge(*got("ql_ready", t, len(t.groups) * (b + 1)))
                        for j in range(4):
                            c = 4 * r + j
                            z = tr(C(0, DC, r, KP * j, KP), ctx_raw[:, DC * c:DC * c + DC], ident[0:KP, 0:KP])
                        z.then_inc(*sig("ct_psum"))

                @staticmethod
                def maxima(t, b):
                    tiles = t.heads // 2
                    for k in range(tiles):
                        for r in range(NPIECE):
                            n = NPIECE * k + r
                            yield 1 + n
                            if n == 0:
                                pe.wait_ge(*got("ctl_ready", t, NPIECE * (b + 1)))
                            if n >= 3:
                                pe.wait_ge(*got("mp_ready", t, NPIECE * tiles * b + n - 2))
                            mm(C(0, 112, r, 0, PIECE), q_hi[0:DC, b, 112 * k:112 * k + 112],
                               ctxT_hi[0:DC, b, PIECE * r:PIECE * r + PIECE], start=True, stop=True)\
                                .then_inc(*sig("mp_psum"))
                    yield 3 * tiles + 3
                    pe.wait_ge(*got("mx_ready", t, b + 1))
                    for k in range(tiles):
                        z = mm(C(DC, 1, k // 4, 112 * (k % 4), 112), mx[:, k:k + 1], ident[0:112, 0:112],
                               start=True, stop=True)
                    z.then_inc(*sig("mr_psum"))

                @staticmethod
                def normalise(t, b, last=False):
                    yield 1
                    pe.wait_ge(*got("u_copied", t, len(t.groups) * (b + 1)))
                    if b == 0:
                        pe.wait_ge(*got("mr_ready", t, 2))
                        pe.wait_ge(*got("xp_ready", t, 0))
                        if not last:
                            pe.wait_ge(*got(*(("xm_ready", t + 1, 1), ("o_ready", t + 1, 1), ("ht_ready", t + 1, 1))[t.ph]))
                    else:
                        pe.wait_ge(*(got("ut_ready", t, 1) if last else got("mr_ready", t, 3)))
                    for k in range(t.heads // 2):
                        z = mm(C(0, 112, 0, k, 1), u_sb[DC:DC + 1, 112 * k:112 * k + 112], ones[DC:DC + 1, 0:1],
                               start=True, stop=True)
                    z.then_inc(*sig("sum_psum"))
                    yield 4
                    pe.wait_ge(*got("diag_ready", t, b + 1))
                    for g, (h0, n) in enumerate(t.groups):
                        z = mm(C(0, DC, g, 0, T * n), ones[0:112, 0:DC], diag[:, T * h0:T * (h0 + n)],
                               start=True, stop=True)
                    z.then_inc(*sig("rb_psum"))

                @staticmethod
                def post(t, last=False):
                    yield 1
                    pe.wait_ge(*got("ut_ready", t, 2))
                    if not last:
                        pe.wait_ge(*got("mr_ready", t, 4))
                    r = C(0, 128, 0, 0, D)
                    if t.ph != 1:
                        mm(r, ones[DC:DC + 1, :], rows[:, D * (2 - t.ph // 2):D * (3 - t.ph // 2)], start=True, stop=False)
                    for h in range(t.heads):
                        z = mm(r, uT[:, h, :, :], w_n[:, h, :], start=(t.ph == 1 and h == 0), stop=(h == t.heads - 1))
                    z.then_inc(*sig("rp_psum"))
                    if t.ph == 1:
                        return
                    yield 4
                    pe.wait_ge(*got("xnf_ready", t, 1))
                    for i in range(2):
                        z = tr(C(0, HF, 1, 128 * i, 128), xnF[:, HF * i:HF * i + HF], ident[:, :])
                    z.then_inc(*sig("xnf_psum"))
                    for c in range(10):
                        if c % 5 == 0:
                            yield 6 + c // 5
                        if c == 0:
                            pe.wait_ge(*got("hf_ready", t, 1))
                        z = both(FC(c), lambda i: fw1[:, i, 128 * c:128 * c + 128], lambda i: hF[:, i, :, :])
                    z.then_inc(*sig("f_psum"))
                    yield 10
                    pe.wait_ge(*got("ff_ready", t, 1))
                    mm(r, ones[DC:DC + 1, :], rows[:, D * (3 - t.ph // 2):D * (4 - t.ph // 2)], start=True, stop=False)
                    for c in range(5):
                        z = mm(r, gT[:, c, :], fw2[:, c, :], start=False, stop=(c == 4))
                    z.then_inc(*sig("rp_psum"))

            def main(t, b):
                G = t.groups
                total = NC * len(G)
                first = total * b

                def scores(n):
                    c, g = divmod(n, len(G))
                    h0, nh = G[g]
                    kp = KP if c < 8 or t.ph != 1 else KP - 1
                    q = slice(T * h0, T * (h0 + nh))
                    k = slice(KP * c, KP * c + kp)
                    dst = ps_s[0:kp, (first + n) % 2, 0:T * nh]
                    pe.wait_ge(*got("exp_done", t, first + n - 1))
                    mm(dst, ctxT_hi[:, b, k], q_hi[:, b, q], start=True, stop=False)
                    mm(dst, ctxT_hi[0:DC, b, k], q_lo[:, b, q], start=False, stop=False)
                    mm(dst, ctxT_lo[:, b, k], q_hi[0:DC, b, q], start=False, stop=True).then_inc(*sig("sc_psum"))

                def outputs(n):
                    c, g = divmod(n, len(G))
                    kp = KP if c < 8 or t.ph != 1 else KP - 1
                    w, s = T * G[g][1], (first + n) % 3
                    pe.wait_ge(*got("pl_ready", t, first + n + 1))
                    if c == 0:
                        pe.wait_ge(*got("u_copied", t, len(G) * (b - 1) + g + 1))
                    dst = ps_u[0:DC + 1, g, 0:w]
                    mm(dst, ctx_hi[0:kp, b, c, :], p_hi[0:kp, s, 0:w], start=(c == 0), stop=False)
                    mm(ps_u[0:DC, g, 0:w], ctx_lo[0:kp, b, c, :], p_hi[0:kp, s, 0:w], start=False, stop=False)
                    mm(dst, ctx_hi[0:kp, b, c, :], p_lo[0:kp, s, 0:w],
                       start=False, stop=(c == NC - 1)).then_inc(*sig("pv_done"))

                for n in range(total + 2):
                    yield 2 * n
                    if n == 0:
                        pe.wait_ge(*got("mr_ready", t, b + 1))
                        pe.wait_ge(*got("ctx_lo", t, b + 1))
                    if n < total:
                        scores(n)
                    yield 2 * n + 1
                    if n >= 2:
                        outputs(n - 2)

            schedule(pe, side, main)

        @block.vector
        def _(dve):
            V = nc.vector

            class side(Idle):
                @staticmethod
                def prologue(ph):
                    if ph == 0:
                        for s, n in (("x_taken", 1), ("cst_ready", 1), ("ut_ready", 2), ("x_handed", 1),
                                     ("xp_ready", 1)):
                            dve.sem_inc(sg[s].sem, n)
                        V.memset(ctxT_hi[DC:DC + 1, :, :].bitcast(F32), 1.0).then_inc(consts, 1)
                    dh, n0 = DH[ph], products_before(ph)
                    for h in range(HEADS[ph]):
                        dve.wait_ge(wt_psum, n0 + h + 1)
                        if n0 + h >= 4:
                            dve.wait_ge(wp_psum, n0 + h - 3)
                        V.tensor_copy(factorT(ph, h), C(0, dh, h % 2, 0, 352)).then_inc(wt_ready, 1)
                    dve.wait_ge(*weights_loaded(ph))
                    dve.wait_ge(consts, N_CONSTS + (ph == 2))

                @staticmethod
                def take(t):
                    dve.wait_ge(*got("x_loaded", t, per("x_loaded", t)))
                    dve.wait_ge(*got("x_handed", t, 0))
                    V.tensor_copy(x_mid[:, :], x_in[:, :]).then_inc(*sig("x_taken"))

                @staticmethod
                def add(t, n, bank):
                    dve.wait_ge(*got("rm_psum", t, n + 1))
                    V.tensor_tensor(x_mid[:, :], x_mid[:, :], C(0, 128, bank, 0, D), ALU.add)\
                        .then_inc(*sig("xm_ready"))

                @staticmethod
                def norm(t, n):
                    if n == 0 and t.ph == 2:
                        dve.wait_ge(*got("x_taken", t, 1))
                    else:
                        dve.wait_ge(*got("xm_ready", t, n + (t.ph == 0)))
                    V.bn_stats(stats[:, :], x_mid[:, :]).then_inc(*sig("ln_stats"))
                    dve.wait_ge(*got("ln_stats", t, n + 1))
                    V.tensor_copy(count[:, :], stats[:, 0:1])
                    V.bn_aggr(mv[:, :], stats[:, :]).then_inc(*sig("ln_mean"))
                    dve.wait_ge(*got("ln_rstd", t, n + 1))
                    V.tensor_scalar(xn[:, :], x_mid[:, :], mv[:, 0:1], rstd[:, :], ALU.subtract, ALU.mult)\
                        .then_inc(*sig("xn_ready"))

                @staticmethod
                def softmax(t, n, src, dst, m, s, axes, half=None):
                    dve.wait_ge(*got("s_psum", t, n + 1))
                    V.tensor_reduce(m, src, AX.X, ALU.max).then_inc(*sig("s_max"))
                    dve.wait_ge(*got("s_max", t, n + 1))
                    V.tensor_tensor(dst, src, m.unsqueeze(axes).broadcast_to(dst.shape), ALU.subtract)\
                        .then_inc(*sig("s_sub"))
                    yield
                    dve.wait_ge(*got("s_exp", t, n + 1))
                    V.tensor_reduce(s, dst, AX.X, ALU.add).then_inc(*sig("s_sum"))
                    dve.wait_ge(*got("s_sum", t, n + 1))
                    V.reciprocal(s, s).then_inc(*sig("s_rec"))
                    k = n + 1 if t.ph else 2 * n + 1
                    dve.wait_ge(*got("s_rec", t, k))
                    if half is not None:
                        V.tensor_scalar(half, half, 0.5, None, ALU.mult).then_inc(*sig("s_rec"))
                        dve.wait_ge(*got("s_rec", t, k + 1))
                    V.tensor_tensor(dst, dst, s.unsqueeze(axes).broadcast_to(dst.shape), ALU.mult)\
                        .then_inc(*sig("p_ready"))
                    yield

                @staticmethod
                def v_blocks(t, vb, bank):
                    for par in range(2):
                        r = slice(S * par, S * par + S)
                        z = V.tensor_copy(vb[r, :, par::2, :], C(S * par, S, bank, 0, 160)
                                          .rearrange("p (b h d) -> p b h d", b=2, h=vb.shape[2] // 2))
                    z.then_inc(*sig("vb_ready"))

                @staticmethod
                def pre(t, first=False):
                    if t.ph == 0:
                        yield from side.pre_0(t)
                    elif t.ph == 1:
                        yield from side.pre_1(t)
                    else:
                        yield from side.pre_2(t)

                @staticmethod
                def pre_0(t):
                    yield 1
                    side.take(t)
                    dve.wait_ge(*got("in_psum", t, 1))
                    V.tensor_copy(csT[:, :, :], C(0, DC, 0, 0, 128).rearrange("p (b s) -> p b s", b=2))\
                        .then_inc(*sig("cst_ready"))
                    yield 3
                    dve.wait_ge(*got("qkv_psum", t, 1))
                    for o in range(2):
                        kk = C(0, HF, 2, 128 * o, 128).rearrange("p (b s) -> p b s", b=2).unsqueeze(2)
                        z = V.tensor_tensor(kb0[:, o, :, :, :], kk.broadcast_to([HF, 2, 4, S]),
                                            hm[:, 0:4].unsqueeze(1).unsqueeze(3).broadcast_to([HF, 2, 4, S]), ALU.mult)
                    z.then_inc(*sig("kb_ready"))
                    side.v_blocks(t, vb0, 0)
                    yield 5
                    s = C(0, 128, 1, 0, 512).rearrange("p (h g w) -> p h g w", h=8, g=4)[:, :, 0:3, :]
                    p = sm[:, 0:512].rearrange("p (h g w) -> p h g w", h=8, g=4)[:, :, 0:3, :]
                    m3, s3 = (v[:, :].rearrange("p (h g) -> p h g", g=3) for v in (smx, ssum))
                    x = side.softmax(t, 0, s, p, m3, s3, 3, half=s3[:, :, 0:3:2])
                    next(x)
                    yield 7
                    next(x)
                    yield 11
                    dve.wait_ge(*got("o_psum", t, 1))
                    V.tensor_copy(oz[:, :], C(0, 128, 0, 0, D)).then_inc(*sig("o_ready"))
                    yield 15
                    side.add(t, 0, 2)
                    side.norm(t, 0)
                    yield 23
                    dve.wait_ge(*got("qkv_psum", t, 3))
                    V.tensor_copy(kb1[S:2 * S, :, 1::2, :].rearrange("p b j s -> p j b s"),
                                  C(S, S, 0, 0, 1280).rearrange("p (j b s) -> p j b s", j=10, b=2))\
                        .then_inc(*sig("kb_ready"))
                    yield 26
                    s = C(0, 128, 0, 0, 1280).rearrange("p (h w) -> p h w", h=20)[:, :, 0:T]
                    x = side.softmax(t, 1, s, smv[:, :, 0:T], smx[:, 0:20], ssum[:, 0:20], 2)
                    next(x)
                    yield 28
                    next(x)
                    for b in range(2):
                        yield 29 + 2 * b
                        dve.wait_ge(*got("qkv_psum", t, 4 + b))
                        V.tensor_copy(kb1[S:2 * S, b, 1::2, :].rearrange("p (f e) d -> p f e d", f=2),
                                      C(S, S, 0, 0, 1024).rearrange("p (f n) -> p f n", f=2)[:, :, 0:320]
                                      .rearrange("p f (e d) -> p f e d", e=5)).then_inc(*sig("vb_ready"))
                    yield 36
                    dve.wait_ge(*got("o_psum", t, 2))
                    V.tensor_copy(qo[:, :], C(0, 128, 0, 0, 1280)).then_inc(*sig("o_ready"))
                    yield 38
                    side.add(t, 1, 0)
                    side.norm(t, 1)

                @staticmethod
                def pre_1(t):
                    yield 1
                    side.take(t)
                    dve.wait_ge(*got("in_psum", t, 1))
                    V.tensor_copy(csT[:, :, :], C(0, DC, 0, 0, 128).rearrange("p (b s) -> p b s", b=2))\
                        .then_inc(*sig("cst_ready"))
                    yield 3
                    dve.wait_ge(*got("qkv_psum", t, 1))
                    V.tensor_copy(caS[:, :], C(0, NCA, 0, 0, 128)).then_inc(*sig("ca_ready"))
                    dve.wait_ge(*got("cst_ready", t, 1))
                    V.tensor_copy(ca_r[:, :, :, :], csT[:, :, 28:32].unsqueeze(2).broadcast_to([DC, 2, 8, NCA]))
                    side.v_blocks(t, vb0, 2)
                    dve.wait_ge(*got("xt_ready", t, 1))
                    for o in range(2):
                        z = V.tensor_tensor(kb0[:, o, :, :, :], hT[:, o, :, :].unsqueeze(2).broadcast_to([HF, 2, 4, S]),
                                            hm[:, 0:4].unsqueeze(1).unsqueeze(3).broadcast_to([HF, 2, 4, S]), ALU.mult)
                    z.then_inc(*sig("kb_ready"))
                    yield 7
                    s = C(0, 128, 0, 0, 512).rearrange("p (h w) -> p h w", h=8)[:, :, 0:T]
                    x = side.softmax(t, 0, s, smv[:, 0:8, 0:T], smx[:, 0:8], ssum[:, 0:8], 2)
                    next(x)
                    yield 9
                    next(x)
                    yield 13
                    dve.wait_ge(*got("o_psum", t, 1))
                    V.tensor_copy(oz[:, :], C(0, 128, 1, 0, D)).then_inc(*sig("o_ready"))
                    yield 17
                    dve.wait_ge(*got("ca_psum", t, 2))
                    for b in range(2):
                        V.tensor_tensor(k2b[:, :, b, :].rearrange("p o (h k) -> p o h k", k=NCA),
                                        C(0, HF, 2, 0, 16).rearrange("p (o b k) -> p o b k", o=2, b=2)[:, :, b, :]
                                        .unsqueeze(2).broadcast_to([HF, 2, 4, NCA]),
                                        hm[:, 0:4].unsqueeze(1).unsqueeze(3).broadcast_to([HF, 2, 4, NCA]), ALU.mult)
                    V.tensor_tensor(v2b[:, :, :], C(0, 32, 0, 0, 320).rearrange("p (b n) -> p b n", b=2),
                                    hm32[:, :].unsqueeze(1).broadcast_to([32, 2, D]), ALU.mult)\
                        .then_inc(*sig("k2_ready"))
                    yield 19
                    s = C(0, 128, 2, 0, 32).rearrange("p (h w) -> p h w", h=8)
                    x = side.softmax(t, 1, s, p2[:, :].rearrange("p (h w) -> p h w", h=8),
                                     smx[:, 0:8], ssum[:, 0:8], 2)
                    next(x)
                    yield 21
                    next(x)
                    yield 25
                    dve.wait_ge(*got("o_psum", t, 2))
                    V.tensor_copy(oz[:, :], C(0, 128, 1, 0, D)).then_inc(*sig("o_ready"))
                    yield 29
                    side.add(t, 0, 1)

                @staticmethod
                def pre_2(t):
                    yield 1
                    side.take(t)
                    side.norm(t, 0)
                    yield 5
                    dve.wait_ge(*got("qkv_psum", t, 1))
                    for o in range(2):
                        for b in range(2):
                            z = V.tensor_tensor(kb3[:, o, b, :, :],
                                                C(0, HF, 2, 128 * o + S * b, S).unsqueeze(1).broadcast_to([HF, 10, S]),
                                                hm[:, 4:14].unsqueeze(2).broadcast_to([HF, 10, S]), ALU.mult)
                    z.then_inc(*sig("kb_ready"))
                    side.v_blocks(t, vb3, 0)
                    yield 8
                    s = C(0, 128, 0, 0, 1280).rearrange("p (h w) -> p h w", h=20)[:, :, 0:T]
                    x = side.softmax(t, 0, s, smv[:, :, 0:T], smx[:, 0:20], ssum[:, 0:20], 2)
                    next(x)
                    yield 10
                    next(x)
                    yield 14
                    dve.wait_ge(*got("o_psum", t, 1))
                    V.tensor_copy(oz[:, :], C(0, 128, 0, 0, D)).then_inc(*sig("o_ready"))
                    yield 18
                    side.add(t, 0, 2)
                    side.norm(t, 1)

                @staticmethod
                def queries(t, b):
                    for g, (h0, n) in enumerate(t.groups):
                        yield 2 + g
                        k = len(t.groups) * b + g + 1
                        dve.wait_ge(*got("qh_ready", t, k))
                        q = slice(T * h0, T * (h0 + n))
                        V.tensor_tensor(q_lo[:, b, q].rearrange("p (h s) -> p h s", h=n),
                                        C(0, DC, g, 0, S * n).rearrange("p (h s) -> p h s", h=n)[:, :, 0:T],
                                        q_hi[0:DC, b, q].bitcast(F32).rearrange("p (h s) -> p h s", h=n),
                                        ALU.subtract).then_inc(*sig("ql_ready"))

                @staticmethod
                def context(t, b):
                    for r in range(NPIECE):
                        yield 2 + r
                        dve.wait_ge(*got("cth_ready", t, NPIECE * b + r + 1))
                        k = slice(PIECE * r, PIECE * r + PIECE)
                        V.tensor_tensor(ctxT_lo[:, b, k], C(0, DC, r, 0, PIECE), ctxT_hi[0:DC, b, k].bitcast(F32),
                                        ALU.subtract).then_inc(*sig("ctl_ready"))

                @staticmethod
                def maxima(t, b):
                    tiles = t.heads // 2
                    for k in range(tiles):
                        for r in range(NPIECE):
                            n = NPIECE * k + r
                            yield 2 + n
                            dve.wait_ge(*got("mp_psum", t, NPIECE * tiles * b + n + 1))
                            if t.ph == 1 and r == NPIECE - 1:
                                z = V.tensor_reduce(mpiece[:, k, r:r + 1], C(0, 112, r, 0, PIECE)
                                                    .rearrange("p (c s) -> p c s", c=4)[:, :, 0:KP - 1], AX.XY, ALU.max)
                            else:
                                z = V.tensor_reduce(mpiece[:, k, r:r + 1], C(0, 112, r, 0, PIECE), AX.X, ALU.max)
                            z.then_inc(*sig("mp_ready"))
                    yield 3 * tiles + 2
                    dve.wait_ge(*got("mp_ready", t, NPIECE * tiles * (b + 1)))
                    V.tensor_reduce(mx[:, 0:tiles], mpiece[:, 0:tiles, :], AX.X, ALU.max).then_inc(*sig("mx_ready"))

                @staticmethod
                def normalise(t, b, last=False):
                    yield 2
                    tiles = t.heads // 2
                    dve.wait_ge(*got("sum_psum", t, b + 1))
                    V.reciprocal(srec[:, 0:tiles], C(0, 112, 0, 0, tiles)).then_inc(*sig("rec_ready"))
                    dve.wait_ge(*got("rec_ready", t, b + 1))
                    V.tensor_tensor(diag[:, 0:112 * tiles].rearrange("p (k q) -> p k q", q=112),
                                    ident[0:112, 0:112].unsqueeze(1).broadcast_to([112, tiles, 112]),
                                    srec[:, 0:tiles].unsqueeze(2).broadcast_to([112, tiles, 112]), ALU.mult)\
                        .then_inc(*sig("diag_ready"))
                    for g, (h0, n) in enumerate(t.groups):
                        yield 5 + g
                        if g == 0:
                            dve.wait_ge(*got("rb_psum", t, b + 1))
                            dve.wait_ge(*got("rp_psum", t, 0))
                        z = V.tensor_tensor(uT[:, h0:h0 + n, b, 0:T],
                                            u_sb[0:DC, T * h0:T * (h0 + n)].rearrange("p (h s) -> p h s", h=n),
                                            C(0, DC, g, 0, T * n).rearrange("p (h s) -> p h s", h=n), ALU.mult)
                    z.then_inc(*sig("ut_ready"))

                @staticmethod
                def hand(t):
                    yield 1
                    dve.wait_ge(*got("xp_ready", t, 0))
                    dve.wait_ge(*got("xm_ready", t, per("xm_ready", t)))
                    V.tensor_copy(x_post[:, :], x_mid[:, :]).then_inc(*sig("x_handed"))

                @staticmethod
                def add_post(t, n):
                    dve.wait_ge(*got("rp_psum", t, n + 1))
                    if n == 0:
                        dve.wait_ge(*got("x_handed", t, 1))
                    final = n + 1 == per("xp_ready", t)
                    if final:
                        dve.wait_ge(*got("x_saved", t, 0))
                    V.tensor_tensor((x_out if final else x_post)[:, :], x_post[:, :], C(0, 128, 0, 0, D), ALU.add)\
                        .then_inc(*sig("xp_ready"))

                @staticmethod
                def post(t, last=False):
                    yield 2
                    side.add_post(t, 0)
                    if t.ph == 1:
                        return
                    dve.wait_ge(*got("xp_ready", t, 1))
                    V.bn_stats(statsF[:, :], x_post[:, :]).then_inc(*sig("lnf_stats"))
                    dve.wait_ge(*got("lnf_stats", t, 1))
                    V.tensor_copy(countF[:, :], statsF[:, 0:1])
                    V.bn_aggr(mvF[:, :], statsF[:, :]).then_inc(*sig("lnf_mean"))
                    yield 3
                    dve.wait_ge(*got("lnf_rstd", t, 1))
                    V.tensor_scalar(xnF[:, :], x_post[:, :], mvF[:, 0:1], rstdF[:, :], ALU.subtract, ALU.mult)\
                        .then_inc(*sig("xnf_ready"))
                    yield 9
                    dve.wait_ge(*got("gelu_ready", t, 1))
                    for c in range(5):
                        z = V.scalar_tensor_tensor(gT[:, c, :], FC(c), bff[:, c:c + 1], gT[:, c, :], ALU.add, ALU.mult)
                    z.then_inc(*sig("ff_ready"))
                    yield 11
                    side.add_post(t, 1)

            def main(t, b):
                return iter(())

            schedule(dve, side, main)

        @block.gpsimd
        def _(pool):
            P = nc.gpsimd
            for tile, v in ((ident, 0.0), (ones, 1.0), (neghalf, -0.5), (eps, EPS), (sm, 0.0), (kvb, 0.0), (vb_s, 0.0), (cs, 0.0),
                            (uT, 0.0)):
                P.memset(tile[tuple(slice(None) for _ in tile.shape)], v).then_inc(consts, 1)
            P.memset(ctx_hi[:, :, :, DC:DC + 1].bitcast(F32), 1.0).then_inc(consts, 1)
            pool.wait_ge(consts, N_CONSTS - 1)
            P.affine_select(out=ident[:, :], in_=ident[:, :], compare_op=ALU.not_equal, fill=1.0,
                            base=0, pattern=[[-1, 128]], channel_multiplier=1).then_inc(consts, 1)

            def rsqrt(t, n, mean, var, out_, names):
                m, v, r = names
                pool.wait_ge(*got(m, t, n + 1))
                P.tensor_tensor(var[:, :], mean[:, 1:2], eps[:, :], ALU.add).then_inc(*sig(v))
                pool.wait_ge(*got(v, t, n + 1))
                P.tensor_tensor(out_[:, :], var[:, :], neghalf[:, :], ALU.pow).then_inc(*sig(r))

            class side(Idle):
                @staticmethod
                def prologue(ph):
                    if ph == 0:
                        pool.sem_inc(sg["ctx_lo"].sem, 1)
                        pool.sem_inc(sg["pl_ready"].sem, 2)
                    if ph == 2:
                        pool.wait_ge(*sg["xp_ready"].end(1))
                        P.memset(vb_s[:, :], 0.0).then_inc(consts, 1)

                @staticmethod
                def pre(t, first=False):
                    names = ("ln_mean", "ln_var", "ln_rstd")
                    if t.ph == 0:
                        yield 15
                        rsqrt(t, 0, mv, ve, rstd, names)
                        yield 38
                        rsqrt(t, 1, mv, ve, rstd, names)
                    if t.ph == 2:
                        yield 1
                        rsqrt(t, 0, mv, ve, rstd, names)
                        yield 18
                        rsqrt(t, 1, mv, ve, rstd, names)

                @staticmethod
                def context(t, b):
                    yield 2
                    pool.wait_ge(*got("ctx_hi", t, b + 1))
                    P.tensor_tensor(ctx_lo[:, b, :, :], ctx_raw[:, :].rearrange("p (c d) -> p c d", c=NC),
                                    ctx_hi[:, b, :, 0:DC].bitcast(F32), ALU.subtract).then_inc(*sig("ctx_lo"))

                @staticmethod
                def post(t, last=False):
                    if t.ph != 1:
                        yield 2
                        rsqrt(t, 0, mvF, veF, rstdF, ("lnf_mean", "lnf_var", "lnf_rstd"))

            def main(t, b):
                G = t.groups
                for n in range(NC * len(G)):
                    yield 2 * n
                    c, g = divmod(n, len(G))
                    kp = KP if c < 8 or t.ph != 1 else KP - 1
                    w, k = T * G[g][1], NC * len(G) * b + n
                    pool.wait_ge(*got("exp_done", t, k + 1))
                    pool.wait_ge(*got("pv_done", t, k - 2))
                    P.tensor_tensor(p_lo[0:kp, k % 3, 0:w], p32[0:kp, k % 2, 0:w],
                                    p_hi[0:kp, k % 3, 0:w].bitcast(F32), ALU.subtract).then_inc(*sig("pl_ready"))

            schedule(pool, side, main)

        @block.scalar
        def _(act):
            A = nc.scalar.activation
            SHORT_SCALE = ((20 ** -0.5, 64 ** -0.5), (20 ** -0.5, 20 ** -0.5), (8 ** -0.5,))

            class side(Idle):
                @staticmethod
                def prologue(ph):
                    if ph == 0:
                        act.sem_inc(sg["exp_done"].sem, 2)
                        act.sem_inc(sg["u_copied"].sem, 3)
                    n0 = products_before(ph)
                    for h in range(HEADS[ph]):
                        act.wait_ge(wp_psum, n0 + h + 1)
                        A(w_m[:, :, DC * h:DC * h + DC],
                          ps_u[0:HF, 1 + h % 2, 0:2 * DC].rearrange("p (a n) -> p a n", a=2), ACT.Copy)
                        A(w_n[:, h, :], ps_u[0:DC, 1 + h % 2, 192:352], ACT.Copy).then_inc(wp_ready, 1)
                    act.wait_ge(*weights_loaded(ph))

                @staticmethod
                def norm(t, n, bank):
                    act.wait_ge(*got("xn_psum", t, n + 1))
                    for i in range(2):
                        z = A(hT[:, i, :, :], C(0, HF, bank, 128 * i, 128).rearrange("p (b s) -> p b s", b=2),
                              ACT.Identity, scale=gb[:, i, 2 * n:2 * n + 1], bias=gb[:, i, 2 * n + 1:2 * n + 2])
                    z.then_inc(*sig("ht_ready"))

                @staticmethod
                def exps(t, n, p):
                    act.wait_ge(*got("s_sub", t, n + 1))
                    A(p, p, ACT.Exp, scale=SHORT_SCALE[t.ph][n]).then_inc(*sig("s_exp"))

                @staticmethod
                def copy(dst, bank, rows_, n, sgn):
                    A(dst, C(0, rows_, bank, 0, n), ACT.Copy).then_inc(*sig(sgn))

                @staticmethod
                def pre(t, first=False):
                    two = "p (a b s) -> p a b s"
                    if t.ph < 2:
                        yield 1
                        act.wait_ge(*got("in_psum", t, 1))
                        A((xT, hT)[t.ph][:, :, :, :], C(0, HF, 1, 0, 256).rearrange(two, a=2, b=2), ACT.Copy)\
                            .then_inc(*sig("xt_ready"))
                    if t.ph == 0:
                        yield 3
                        act.wait_ge(*got("qkv_psum", t, 1))
                        A(q_small[:, :, :, :], C(0, HF, 1, 0, 256).rearrange(two, a=2, b=2), ACT.Copy)\
                            .then_inc(*sig("q_ready"))
                        yield 6
                        side.exps(t, 0, sm[:, 0:512].rearrange("p (h w) -> p h w", h=8)[:, :, 0:48])
                        yield 9
                        act.wait_ge(*got("pt_psum", t, 1))
                        A(pT[:, 0:512], C(0, 128, 2, 0, 512), ACT.Copy).then_inc(*sig("pt_ready"))
                        yield 13
                        act.wait_ge(*got("ot_psum", t, 1))
                        A(xT[:, :, :, :], C(0, HF, 1, 0, 256).rearrange(two, a=2, b=2), ACT.Copy)\
                            .then_inc(*sig("ot_ready"))
                        yield 17
                        side.norm(t, 0, 0)
                        yield 20
                        act.wait_ge(*got("qkv_psum", t, 2))
                        A(qo[:, :], C(0, 128, 0, 0, 1280), ACT.Copy).then_inc(*sig("q_ready"))
                        yield 23
                        act.wait_ge(*got("qkv_psum", t, 3))
                        A(kb1[0:S, :, 0::2, :].rearrange("p b j s -> p j b s"),
                          C(0, S, 0, 0, 1280).rearrange("p (j b s) -> p j b s", j=10, b=2), ACT.Copy)\
                            .then_inc(*sig("kb2_ready"))
                        yield 27
                        side.exps(t, 1, smv[:, :, 0:T])
                        for b in range(2):
                            yield 29 + 2 * b
                            act.wait_ge(*got("qkv_psum", t, 4 + b))
                            A(kb1[0:S, b, 0::2, :].rearrange("p (f e) d -> p f e d", f=2),
                              C(0, S, 0, 0, 1024).rearrange("p (f n) -> p f n", f=2)[:, :, 0:320]
                              .rearrange("p f (e d) -> p f e d", e=5), ACT.Copy).then_inc(*sig("vb2_ready"))
                        yield 33
                        act.wait_ge(*got("pt_psum", t, 2))
                        A(pT[:, :], C(0, 128, 0, 0, 1280), ACT.Copy).then_inc(*sig("pt_ready"))
                        yield 40
                        side.norm(t, 1, 1)
                    elif t.ph == 1:
                        yield 5
                        act.wait_ge(*got("ca_psum", t, 1))
                        A(q_small[:, :, :, :], C(0, HF, 1, 0, 256).rearrange(two, a=2, b=2), ACT.Copy)\
                            .then_inc(*sig("q_ready"))
                        yield 8
                        side.exps(t, 0, smv[:, 0:8, 0:T])
                        yield 11
                        act.wait_ge(*got("pt_psum", t, 1))
                        A(pT[:, 0:512], C(0, 128, 2, 0, 512), ACT.Copy).then_inc(*sig("pt_ready"))
                        yield 15
                        act.wait_ge(*got("ot_psum", t, 1))
                        A(xT[:, :, :, :], C(0, HF, 0, 0, 256).rearrange(two, a=2, b=2), ACT.Copy)\
                            .then_inc(*sig("ot_ready"))
                        yield 17
                        act.wait_ge(*got("ca_psum", t, 2))
                        A(q_small[:, :, :, :], C(0, HF, 1, 0, 256).rearrange(two, a=2, b=2), ACT.Copy)\
                            .then_inc(*sig("q_ready"))
                        yield 20
                        side.exps(t, 1, p2[:, :])
                        yield 23
                        act.wait_ge(*got("pt_psum", t, 2))
                        A(pT[0:32, 0:128], C(0, 32, 0, 0, 128), ACT.Copy).then_inc(*sig("pt_ready"))
                        yield 27
                        act.wait_ge(*got("ot_psum", t, 2))
                        A(xT[:, :, :, :], C(0, HF, 0, 0, 256).rearrange(two, a=2, b=2), ACT.Copy)\
                            .then_inc(*sig("ot_ready"))
                    else:
                        yield 3
                        side.norm(t, 0, 0)
                        yield 5
                        act.wait_ge(*got("qkv_psum", t, 1))
                        A(q_small[:, :, :, :], C(0, HF, 1, 0, 256).rearrange(two, a=2, b=2), ACT.Copy)\
                            .then_inc(*sig("q_ready"))
                        yield 9
                        side.exps(t, 0, smv[:, :, 0:T])
                        yield 12
                        act.wait_ge(*got("pt_psum", t, 1))
                        A(pT[:, :], C(0, 128, 0, 0, 1280), ACT.Copy).then_inc(*sig("pt_ready"))
                        yield 16
                        act.wait_ge(*got("ot_psum", t, 1))
                        A(xT[:, :, :, :], C(0, HF, 1, 0, 256).rearrange(two, a=2, b=2), ACT.Copy)\
                            .then_inc(*sig("ot_ready"))
                        yield 20
                        side.norm(t, 1, 0)

                @staticmethod
                def queries(t, b):
                    for g, (h0, n) in enumerate(t.groups):
                        yield 1 + g
                        if g == 0:
                            act.wait_ge(*got("pv_done", t, per("pv_done", t) // 2 * (b - 1)))
                        act.wait_ge(*got("qt_psum", t, len(t.groups) * b + g + 1))
                        q = slice(T * h0, T * (h0 + n))
                        A(q_hi[0:DC, b, q].rearrange("p (h s) -> p h s", h=n),
                          C(0, DC, g, 0, S * n).rearrange("p (h s) -> p h s", h=n)[:, :, 0:T], ACT.Copy)\
                            .then_inc(*sig("qh_ready"))

                @staticmethod
                def context(t, b):
                    yield 1
                    act.wait_ge(*got("cr_loaded", t, 16 * (b + 1)))
                    A(ctx_hi[:, b, :, 0:DC], ctx_raw[:, :].rearrange("p (c d) -> p c d", c=NC), ACT.Copy)\
                        .then_inc(*sig("ctx_hi"))
                    for r in range(NPIECE):
                        yield 1 + r
                        act.wait_ge(*got("ct_psum", t, NPIECE * b + r + 1))
                        A(ctxT_hi[0:DC, b, PIECE * r:PIECE * r + PIECE], C(0, DC, r, 0, PIECE), ACT.Copy)\
                            .then_inc(*sig("cth_ready"))

                @staticmethod
                def maxima(t, b):
                    yield 3 * t.heads // 2 + 4
                    act.wait_ge(*got("mr_psum", t, b + 1))
                    for g, (h0, n) in enumerate(t.groups):
                        z = A(q_hi[DC:DC + 1, b, T * h0:T * (h0 + n)], C(DC, 1, g, 0, T * n), ACT.Copy, scale=-1.0)
                    z.then_inc(*sig("mr_ready"))

                @staticmethod
                def post(t, last=False):
                    if t.ph == 1:
                        return
                    yield 5
                    act.wait_ge(*got("xnf_psum", t, 1))
                    for i in range(2):
                        z = A(hF[:, i, :, :], C(0, HF, 1, 128 * i, 128).rearrange("p (b s) -> p b s", b=2),
                              ACT.Identity, scale=gb[:, i, 4:5], bias=gb[:, i, 5:6])
                    z.then_inc(*sig("hf_ready"))
                    yield 8
                    act.wait_ge(*got("f_psum", t, 1))
                    for c in range(5):
                        z = A(gT[:, c, :], FC(5 + c), ACT.Gelu_apprx_tanh if t.ph == 0 else ACT.Gelu,
                              bias=bff[:, 5 + c:6 + c])
                    z.then_inc(*sig("gelu_ready"))

            def main(t, b):
                G = t.groups
                total = NC * len(G)
                for n in range(total):
                    yield 2 * n
                    c, g = divmod(n, len(G))
                    kp = KP if c < 8 or t.ph != 1 else KP - 1
                    w, k = T * G[g][1], total * b + n
                    act.wait_ge(*got("sc_psum", t, k + 1))
                    act.wait_ge(*got("pl_ready", t, k - 1))
                    A(p32[0:kp, k % 2, 0:w], ps_s[0:kp, k % 2, 0:w], ACT.Exp, scale=DH[t.ph] ** -0.5)
                    act.wait_ge(*got("pv_done", t, k - 2))
                    A(p_hi[0:kp, k % 3, 0:w], ps_s[0:kp, k % 2, 0:w], ACT.Exp, scale=DH[t.ph] ** -0.5)\
                        .then_inc(*sig("exp_done"))
                yield 2 * total
                act.wait_ge(*got("ut_ready", t, b))
                for g, (h0, nh) in enumerate(G):
                    act.wait_ge(*got("pv_done", t, total * b + total - len(G) + g + 1))
                    A(u_sb[:, T * h0:T * (h0 + nh)], ps_u[0:DC + 1, g, 0:T * nh], ACT.Copy)\
                        .then_inc(*sig("u_copied"))

            schedule(act, side, main)

        wrong = {}
        for name, s in sg.items():
            if name.endswith(("_loaded", "_saved")):
                continue
            seen = tuple(s.seen.get(ph, 0) for ph in range(3))
            if seen != s.counts:
                wrong[name] = (seen, s.counts)
        assert not wrong, wrong


def kernel(**inputs):
    import concourse.bacc as bacc
    from concourse.bass_utils import run_bass_kernel_spmd

    nc = bacc.Bacc("TRN2", target_bir_lowering=False, num_devices=1)
    arrays, args = {}, {}

    def give(name, v):
        v = np.ascontiguousarray(v)
        arrays[f"in_{name}"] = v
        return nc.dram_tensor(f"in_{name}", v.shape, mybir.dt.from_np(v.dtype), kind="ExternalInput").ap()

    for name, v in inputs.items():
        args[name] = give(name, v)
    sel = np.zeros((DC, S), np.float32)
    chosen = np.linspace(0, DC - 1, T).astype(np.int64)
    sel[chosen, np.arange(T)] = 1.0
    f = np.arange(HF)
    hmask = np.concatenate([f[:, None] // 20 == np.arange(4), f[:, None] // 8 == np.arange(10)], 1)
    hmask32 = np.arange(32)[:, None] // NCA == np.arange(D) // 20
    consts = [give(n, v.astype(np.float32)) for n, v in (("sel", sel), ("hmask", hmask), ("hmask32", hmask32))]
    out = nc.dram_tensor("out", (B, T, D), F32, kind="ExternalOutput").ap()
    xattn_stack(nc, args, *consts, out)
    r = run_bass_kernel_spmd(nc, [arrays], core_ids=[0])
    return r.results[0]["out"]
```

```python
from contextlib import ExitStack

import numpy as np
import concourse.bass as bass
from concourse import mybir

F32 = mybir.dt.float32
F32R = mybir.dt.float32r
ACT = mybir.ActivationFunctionType
ALU = mybir.AluOpType
AX = mybir.AxisListType

B, T, D = 32, 56, 160
KEYS, DC = 1500, 96
PAIRS = B // 2
S = 64
NC = 12
KP = KEYS // NC
HF = D // 2
EPS = 1e-5
PIECE = 4 * KP
NPIECE = KEYS // PIECE
HEADS = (20, 8, 20)
DH = (64, 20, 8)
CROSS_KEYS = (KEYS, KEYS - 4, KEYS)
NCA = 4
FF = 640


def groups(heads):
    return [(h, min(8, heads - h)) for h in range(0, heads, 8)]


class Signal:

    def __init__(self, sem, name, counts, credit):
        self.sem, self.name, self.counts, self.credit = sem, name, counts, credit
        self.seen = {}

    def __call__(self, t, k):
        before = self.credit + PAIRS * sum(self.counts[:t.ph])
        return self.sem, t.it * self.counts[t.ph] + (before + k)

    def end(self, ph):
        return self.sem, self.credit + PAIRS * sum(self.counts[:ph + 1])


class At:

    def __init__(self, ph, it, ahead=False):
        self.ph, self.it, self.ahead = ph, it, ahead
        self.heads = HEADS[ph]
        self.groups = groups(self.heads)

    def __add__(self, n):
        return At(self.ph, self.it + n)


COUNTS = {
    "x_loaded": ((64, 16, 16), 0), "cs_loaded": ((96, 96, 0), 0), "cr_loaded": ((32, 32, 32), 0),
    "x_saved": ((16, 16, 32), 1),
    "x_taken": ((1, 1, 1), 1), "x_handed": ((1, 1, 1), 1),
    "in_psum": ((1, 1, 0), 0), "cst_ready": ((1, 1, 0), 1), "xt_ready": ((1, 1, 0), 0),
    "ln_stats": ((2, 0, 2), 0), "ln_mean": ((2, 0, 2), 0), "ln_var": ((2, 0, 2), 0), "ln_rstd": ((2, 0, 2), 0),
    "xn_ready": ((2, 0, 2), 0), "xn_psum": ((2, 0, 2), 0), "ht_ready": ((2, 0, 2), 0),
    "qkv_psum": ((5, 1, 1), 0), "q_ready": ((2, 2, 1), 0), "kb_ready": ((2, 1, 1), 0), "kb2_ready": ((1, 0, 0), 0),
    "vb_ready": ((3, 1, 1), 0), "vb2_ready": ((2, 0, 0), 0),
    "ca_psum": ((0, 2, 0), 0), "ca_ready": ((0, 1, 0), 0), "k2_ready": ((0, 1, 0), 0),
    "s_psum": ((2, 2, 1), 0), "s_max": ((2, 2, 1), 0), "s_sub": ((2, 2, 1), 0), "s_exp": ((2, 2, 1), 0),
    "s_sum": ((2, 2, 1), 0), "s_rec": ((3, 2, 1), 0), "p_ready": ((2, 2, 1), 0),
    "pt_psum": ((2, 2, 1), 0), "pt_ready": ((2, 2, 1), 0), "o_psum": ((2, 2, 1), 0), "o_ready": ((2, 2, 1), 0),
    "ot_psum": ((1, 2, 1), 0), "ot_ready": ((1, 2, 1), 0), "rm_psum": ((2, 1, 1), 0), "xm_ready": ((2, 1, 1), 0),
    "qt_psum": ((6, 2, 6), 0), "qh_ready": ((6, 2, 6), 0), "ql_ready": ((6, 2, 6), 0),
    "ctx_hi": ((2, 2, 2), 0), "ctx_lo": ((2, 2, 2), 1),
    "ct_psum": ((6, 6, 6), 1), "cth_ready": ((6, 6, 6), 0), "ctl_ready": ((6, 6, 6), 0),
    "mp_psum": ((60, 24, 60), 0), "mp_ready": ((60, 24, 60), 0), "mx_ready": ((2, 2, 2), 0),
    "mr_psum": ((2, 2, 2), 0), "mr_ready": ((2, 2, 2), 0),
    "sc_psum": ((72, 24, 72), 0), "exp_done": ((72, 24, 72), 2),     "pl_ready": ((72, 24, 72), 2), "pv_done": ((72, 24, 72), 36),
    "u_copied": ((6, 2, 6), 3),
    "sum_psum": ((2, 2, 2), 0), "rec_ready": ((2, 2, 2), 0), "diag_ready": ((2, 2, 2), 0),
    "rb_psum": ((2, 2, 2), 0), "ut_ready": ((2, 2, 2), 2),
    "rp_psum": ((2, 1, 2), 1), "xp_ready": ((2, 1, 2), 1),
    "lnf_stats": ((1, 0, 1), 0), "lnf_mean": ((1, 0, 1), 0), "lnf_var": ((1, 0, 1), 0), "lnf_rstd": ((1, 0, 1), 0),
    "xnf_ready": ((1, 0, 1), 0), "xnf_psum": ((1, 0, 1), 0), "hf_ready": ((1, 0, 1), 0),
    "f_psum": ((1, 0, 1), 0), "gelu_ready": ((1, 0, 1), 0), "ff_ready": ((1, 0, 1), 0),
}


class Idle:

    @staticmethod
    def nothing(t, b=0, last=False):
        return iter(())

    pre = queries = context = maxima = normalise = hand = post = nothing


def xattn_stack(nc, a, sel, hmask, hmask32, out):
    es = ExitStack()
    with es:
        def sb(name, shape, dt=F32):
            return es.enter_context(nc.sbuf_tensor(name, shape, dt))

        w_area = sb("w_area", [128, 7680])
        w_o = sb("w_o", [128, 1600])
        w_m = sb("w_m", [HF, 2, 20 * DC])
        w_n = sb("w_n", [DC, 20, D])
        w_ff = sb("w_ff", [128, 3360])
        w_s = sb("w_s", [128, 1280])
        gb = sb("gb", [HF, 2, 8])
        bff = sb("bff", [128, 10])
        ident = sb("ident", [128, 128])
        ones = sb("ones", [128, 128])
        selc = sb("selc", [DC, S])
        hm = sb("hm", [HF, 14])
        hm32 = sb("hm32", [32, D])
        neghalf = sb("neghalf", [128, 1])
        eps = sb("eps", [128, 1])
        count = sb("count", [128, 1])
        countF = sb("countF", [128, 1])
        ctx_raw = sb("ctx_raw", [KP, NC * DC])
        ctx_hi = sb("ctx_hi", [KP, 2, NC, DC + 1], F32R)
        ctx_lo = sb("ctx_lo", [KP, 2, NC, DC], F32R)
        ctxT_hi = sb("ctxT_hi", [DC + 1, 2, KEYS], F32R)
        ctxT_lo = sb("ctxT_lo", [DC, 2, KEYS], F32R)
        q_hi = sb("q_hi", [DC + 1, 2, 20 * T], F32R)
        q_lo = sb("q_lo", [DC, 2, 20 * T], F32R)
        p32 = sb("p32", [KP, 2, 448])
        p_hi = sb("p_hi", [KP, 3, 448], F32R)
        p_lo = sb("p_lo", [KP, 3, 448], F32R)
        uT = sb("uT", [DC, 20, 2, S])
        mpiece = sb("mpiece", [112, 10, NPIECE])
        mx = sb("mx", [112, 10])
        srec = sb("srec", [112, 10])
        x_in = sb("x_in", [128, D])
        x_mid = sb("x_mid", [128, D])
        x_post = sb("x_post", [128, D])
        x_out = sb("x_out", [128, D])
        hF = sb("hF", [HF, 2, 2, S])
        xnF = sb("xnF", [128, D])
        statsF = sb("statsF", [128, 6])
        mvF = sb("mvF", [128, 2])
        veF = sb("veF", [128, 1])
        rstdF = sb("rstdF", [128, 1])
        cs = sb("cs", [128, DC])
        csT = sb("csT", [DC, 2, S])
        xT = sb("xT", [HF, 2, 2, S])
        hT = sb("hT", [HF, 2, 2, S])
        xn = sb("xn", [128, D])
        stats = sb("stats", [128, 6])
        mv = sb("mv", [128, 2])
        ve = sb("ve", [128, 1])
        rstd = sb("rstd", [128, 1])
        qo = sb("qo", [128, 10 * 128])
        kvb = sb("kvb", [128, 2 * 20 * 64])
        vb_s = sb("vb_s", [128, 320])
        sm = sb("sm", [128, 20 * S])
        pT = sb("pT", [128, 10 * 128])
        oz = sb("oz", [128, D])
        smx = sb("smx", [128, 24])
        ssum = sb("ssum", [128, 24])
        ca_r = sb("ca_r", [DC, 2, 8, NCA])

        ps_s = es.enter_context(nc.psum_tensor("ps_s", [128, 2, 512], F32))
        ps_u = es.enter_context(nc.psum_tensor("ps_u", [128, 3, 512], F32))
        ps_c = es.enter_context(nc.psum_tensor("ps_c", [128, 1536], F32))

        sg = {n: Signal(es.enter_context(nc.semaphore(n)), n, c, cr) for n, (c, cr) in COUNTS.items()}
        f_loaded = es.enter_context(nc.semaphore("f_loaded"))
        w_loaded = es.enter_context(nc.semaphore("w_loaded"))
        l_loaded = es.enter_context(nc.semaphore("l_loaded"))
        consts = es.enter_context(nc.semaphore("consts"))
        wt_psum = es.enter_context(nc.semaphore("wt_psum"))
        wt_ready = es.enter_context(nc.semaphore("wt_ready"))
        wp_psum = es.enter_context(nc.semaphore("wp_psum"))
        wp_ready = es.enter_context(nc.semaphore("wp_ready"))
        scratch = nc.dram_tensor("x_between", (PAIRS, 128, D), F32, kind="Internal").ap()

        fw1 = w_ff[0:HF, 0:2560].rearrange("p (a n) -> p a n", a=2)
        fw2 = w_ff[:, 2560:3360].rearrange("p (c n) -> p c n", c=5)
        wo_stage = w_ff[:, 0:3200].rearrange("p (h n) -> p h n", n=D)
        qo3 = qo[:, :].rearrange("p (j s) -> p j s", j=10)
        q_small = qo[0:HF, 1024:1280].rearrange("p (a b s) -> p a b s", a=2, b=2)
        p2 = sm[:, 1024:1056]
        k2b = hF[:, 0, :, :].rearrange("p b s -> p (b s)")[:, 0:64].rearrange("p (o b k) -> p o b k", o=2, b=2)
        u_sb = qo[0:DC + 1, 0:20 * T]
        diags = (pT[0:112, 0:20 * T], kvb[0:112, 1024:1024 + 8 * T], pT[0:112, 0:20 * T])
        caS = pT[0:NCA, 832:960]
        v2b = pT[0:32, 512:832].rearrange("p (b n) -> p b n", b=2)
        rows = (w_s[DC:DC + 1, 0:4 * D], w_s[DC:DC + 1, 4 * D:8 * D], w_s[DC:DC + 1, 0:4 * D])
        kb0 = qo[0:HF, 0:1024].rearrange("p (a b h s) -> p a b h s", a=2, b=2, h=4)
        kb2 = kvb[0:HF, 0:1024].rearrange("p (a b h s) -> p a b h s", a=2, b=2, h=4)
        kb1 = kvb[:, :].rearrange("p (b h s) -> p b h s", b=2, h=20)
        kb3 = kvb[0:HF, :].rearrange("p (a b h s) -> p a b h s", a=2, b=2, h=10)
        vb0 = vb_s[:, :].rearrange("p (b h d) -> p b h d", b=2, h=8)
        vb3 = vb_s[:, :].rearrange("p (b h d) -> p b h d", b=2, h=20)
        pT3 = pT[:, :].rearrange("p (k s) -> p k s", s=128)
        gT = pT[:, 0:640].rearrange("p (c s) -> p c s", c=5)
        smv = sm[:, :].rearrange("p (h s) -> p h s", s=S)

        def C(first, n_rows, bank, lo, n):
            return ps_c[first:first + n_rows, 512 * bank + lo:512 * bank + lo + n]

        def FC(c):
            return C(0, 128, *((2, 128 * c) if c < 4 else (1, 128) if c == 4 else (0, 128 * c - 640) if c < 9
                               else (1, 0)), 128)

        def E(first, n_rows, bank, lo, n):
            if bank == 2:
                return C(first, n_rows, 2, lo, n)
            return ps_u[first:first + n_rows, 1 + bank, lo:lo + n]

        def banks(t):
            return 2 if t.ph == 1 else 3

        def side_banks(t):
            return E if t.ph == 1 and not t.ahead else C

        N_CONSTS = 12
        l0_wq = w_s[0:HF, 0:320].rearrange("p (a n) -> p a n", a=2)
        l0_wout = w_s[0:HF, 320:640].rearrange("p (a n) -> p a n", a=2)
        l0_wk = [w_s[0:DC, 640:800], w_s[0:DC, 800:960]]
        l0_wv = [w_s[0:DC, 960:1120], w_s[0:DC, 1120:1280]]
        l2_wqca = w_s[0:NCA, 640:800]
        l2_wkca = w_s[0:DC, 800:960]
        l2_wvca = w_s[0:DC, 960:1120]
        l1_w = [w_area[0:HF, 2560 * i:2560 * i + 2560].rearrange("p (a n) -> p a n", a=2) for i in range(3)]
        l3_w = [w_o[0:HF, 320 * i:320 * i + 320].rearrange("p (a n) -> p a n", a=2) for i in range(3)]
        l3_o = w_o[0:HF, 960:1280].rearrange("p (a n) -> p a n", a=2)
        l1_wo = w_o[:, :].rearrange("p (j n) -> p j n", j=10)

        FACTORS = (("L1_xattn_wq2", "L1_xattn_wk2", "L1_xattn_wv2", "L1_xattn_wo2"),
                   ("L2_xattn_Wq", "L2_xattn_Wk", "L2_xattn_Wv", "L2_xattn_Wout"),
                   ("L3_xattn_q2", "L3_xattn_k2", "L3_xattn_v2", "L3_xattn_o2_w"))

        def factor_views(ph):
            n = HEADS[ph] * DH[ph]
            fq = w_area[0:HF, 0:2 * n].rearrange("p (a n) -> p a n", a=2)
            fk = w_area[0:DC, 2 * n:3 * n]
            fv = w_area[0:DC, 3 * n:4 * n]
            fo = wo_stage if ph == 0 else w_area[:, 4 * n:4 * n + HEADS[ph] * D].rearrange("p (h n) -> p h n", n=D)
            fo = fo[0:DH[ph], 0:HEADS[ph], :]
            return fq, fk, fv, fo

        def factorT(ph, h):
            return w_area[0:DH[ph], 5120 + 352 * (h % 4):5120 + 352 * (h % 4) + 352]

        LN = ((("L1_xattn_g1", "L1_xattn_be1"), ("L1_xattn_g2", "L1_xattn_be2"), ("L1_xattn_g3", "L1_xattn_be3")),
              (),
              (("L3_xattn_n1_g", "L3_xattn_n1_b"), ("L3_xattn_n2_g", "L3_xattn_n2_b"),
               ("L3_xattn_n3_g", "L3_xattn_n3_b")))
        BIAS = (("L0_xattn_b_out", "L1_xattn_bo1", "L1_xattn_bo2", "L1_xattn_b_ff2"),
                ("L2_xattn_b_out",),
                ("L3_xattn_o1_b", "L3_xattn_o2_b", "L3_xattn_ff_b2"))
        FFW = (("L1_xattn_w_ff1", "L1_xattn_b_ff1", "L1_xattn_w_ff2"), (),
               ("L3_xattn_ff_w1", "L3_xattn_ff_b1", "L3_xattn_ff_w2"))

        def halves(ap):
            return ap.rearrange("(a p) n -> p a n", a=2)

        def column(ap, n):
            return ap.rearrange("(a p o) -> p a o", a=n, o=1)

        def first_loads(ph):
            fq, fk, fv, fo = factor_views(ph)
            q, k, v, o = FACTORS[ph]
            return [(fq, halves(a[q])), (fk, a[k]), (fv, a[v]),
                    (fo, a[o].rearrange("(h d) n -> d h n", h=HEADS[ph]))]

        def other_loads(ph):
            r = [(rows[ph][:, D * i:D * i + D], a[n].rearrange("(o n) -> o n", o=1)) for i, n in enumerate(BIAS[ph])]
            for i, (g, b) in enumerate(LN[ph]):
                r += [(gb[:, :, 2 * i:2 * i + 1], column(a[g], 2)), (gb[:, :, 2 * i + 1:2 * i + 2], column(a[b], 2))]
            if ph == 0:
                r += [(l0_wq, halves(a["L0_xattn_w_q"])), (l0_wout, halves(a["L0_xattn_w_out"])),
                      (l0_wk[0], a["L0_xattn_w_k_dis"]), (l0_wk[1], a["L0_xattn_w_k"]),
                      (l0_wv[0], a["L0_xattn_w_v_dis"]), (l0_wv[1], a["L0_xattn_w_v"]),
                      (selc[:, :], sel), (hm[:, :], hmask), (hm32[:, :], hmask32),
                      (l1_wo, a["L1_xattn_wo1"].rearrange("(j p) n -> p j n", j=10))]
            if ph == 1:
                r += [(l0_wq, halves(a["L2_xattn_Wq"])), (l0_wout, halves(a["L2_xattn_Wout"])),
                      (l2_wqca, a["L2_xattn_Wq_ca"]), (l2_wkca, a["L2_xattn_Wk_ca"]), (l2_wvca, a["L2_xattn_Wv_ca"])]
            if ph == 2:
                r += [(l3_w[0], halves(a["L3_xattn_q1"])), (l3_w[1], halves(a["L3_xattn_k1"])),
                      (l3_w[2], halves(a["L3_xattn_v1"])), (l3_o, halves(a["L3_xattn_o1_w"]))]
            if ph != 1:
                r += [(bff[:, :].unsqueeze(2), a[FFW[ph][1]].rearrange("(c p o) -> p c o", c=10, o=1))]
            if ph == 2:
                r += ff_loads(2)
            return r

        def ff_loads(ph):
            w1, _, w2 = FFW[ph]
            return [(fw1, halves(a[w1])), (fw2, a[w2].rearrange("(c p) n -> p c n", c=5))]

        def late_loads():
            return [(l1_w[i], halves(a[n])) for i, n in enumerate(("L1_xattn_wq1", "L1_xattn_wk1", "L1_xattn_wv1"))]\
                + ff_loads(0)

        FIRST = [len(first_loads(ph)) for ph in range(3)]
        OTHER = [len(other_loads(ph)) for ph in range(3)]

        def factors_loaded(ph):
            return f_loaded, 16 * sum(FIRST[:ph + 1])

        def weights_loaded(ph):
            return w_loaded, 16 * sum(OTHER[:ph + 1])

        def late_loaded():
            return l_loaded, 16 * len(late_loads())

        def products_before(ph):
            return sum(HEADS[:ph])

        now = {"ph": 0, "count": False}

        def got(name, t, k):
            return sg[name](t, k)

        def sig(name):
            if now["count"]:
                sg[name].seen[now["ph"]] = sg[name].seen.get(now["ph"], 0) + 1
            return sg[name].sem, 1

        def per(name, t):
            return sg[name].counts[t.ph]

        PARTS = {
            "pre": ((40, 3, {7: 0.5, 16: 1, 22: 2, 27: 2, 34: 1, 35: 0.5, 37: 1, 38: 1.5, 39: 1}), (29, 3.5, {5: 2, 15: 1.5, 22: 0.5, 23: 2}), (20, 2.5, {6: 1.5, 19: 1})),
            "queries": ((4, 1, {}), (2, 3, {}), (4, 1, {2: 1.5})),
            "context": ((4, 1, {}), (4, 4, {}), (4, 1.5, {})),
            "maxima": ((34, 2.5, {}), (16, 3, {}), (34, 2, {})),
            "normalise": ((7, 2, {}), (5, 2, {}), (7, 2, {6: 0.5})),
            "post": ((15, 3, {}), (2, 1.5, {}), (15, 3, {})),
            "hand": ((1, 1, {}), (1, 1, {}), (1, 1, {})),
        }
        LEAD = {"queries": 4, "normalise": 5}
        CUT = (15, 17, 3)
        REST = 30

        def schedule(eng, side, main):
            def part(name, step, *args, last=None, **kw):
                length, weight, extra = PARTS[name][args[0].ph]

                def position(number):
                    return weight * (number + sum(e for k, e in extra.items() if k <= number))

                if last is not None:
                    kw["last"] = last
                return step(*args, **kw), position, position(length), LEAD.get(name, 0)

            def cut(steps, position, length, lead, last):
                pending = []

                def head():
                    number = next(steps, None)
                    while number is not None and number <= last:
                        yield number
                        number = next(steps, None)
                    pending.append(number)

                def tail():
                    number = pending[0]
                    while number is not None:
                        yield number
                        number = next(steps, None)

                return ((head(), position, position(last), 0),
                        (tail(), lambda n: position(n) - position(last), length - position(last), 0))

            def before(t, b):
                return [part("queries", side.queries, t, b), part("context", side.context, t, b),
                        part("maxima", side.maxima, t, b)]

            def lane(parts, start=0.0):
                slots = 2 * NC * len(groups(HEADS[now["ph"]])) - start
                total = sum(length for _, _, length, _ in parts)
                pads, before_it = [], 0
                for _, _, length, lead in parts:
                    pads.append(max(0, (lead - start) * total - slots * before_it) / (slots + start - lead))
                    before_it += length
                scale = slots / max(1, total + sum(pads))
                placed = []
                for (f, position, length, _), pad in zip(parts, pads):
                    start += scale * pad
                    placed.append((f, position, start))
                    start += scale * length
                starts = [p[2] for p in placed] + [start]

                def positions():
                    for f, position, at in placed:
                        for number in f:
                            yield at + scale * position(number)

                return positions(), starts

            def weave(steps, *lanes):
                lanes = [positions for positions, _ in lanes]
                due = [next(x, None) for x in lanes]

                def advance(until=None):
                    while True:
                        ahead = [(at, k) for k, at in enumerate(due) if at is not None]
                        if not ahead or (until is not None and min(ahead)[0] > until):
                            return
                        k = min(ahead)[1]
                        due[k] = next(lanes[k], None)

                for n in steps:
                    if n:
                        advance(n)
                advance()

            def pair(t, first=False, last=False):
                norm = [] if first else [part("normalise", side.normalise, t + (-1), 1, last=False)]
                parts = before(t, 1)
                parts[1:1] = norm
                end = [] if first else [part("post", side.post, t + (-1))]
                end += [part("hand", side.hand, t)]
                if not last:
                    pre_a, pre_b = cut(*part("pre", side.pre, t + 1), CUT[t.ph])
                    end += [pre_a]
                if t.ph == 1:
                    beside, starts = lane(parts)
                    weave(main(t, 0, first=first), (beside, starts), lane(end, starts[2 if norm else 1]))
                else:
                    weave(main(t, 0, first=first), lane(parts + end))
                parts = [part("normalise", side.normalise, t, 0, last=last)]
                if t.ph == 1 and not last:
                    beside, starts = lane(parts + [(iter(()), None, REST, 0)])
                    q, c, m = before(t + 1, 0)
                    weave(main(t, 1, last=last), (beside, starts), lane([pre_b, q[:3] + (starts[1],), c, m]))
                else:
                    if not last:
                        parts += [pre_b] + before(t + 1, 0)
                    elif t.ph < 2:
                        parts += [part("pre", side.pre, At(t.ph + 1, 0, ahead=True))]
                    weave(main(t, 1, last=last), lane(parts))

            for ph in range(3):
                now.update(ph=ph)
                side.prologue(ph)
                t = At(ph, 0)
                weave(iter(()), lane(([] if ph else [part("pre", side.pre, t, first=True)]) + before(t, 0)))
                pair(t, first=True)
                with eng.Fori(1, PAIRS - 1) as it:
                    now.update(count=True)
                    pair(At(ph, it))
                    now.update(count=False)
                pair(At(ph, PAIRS - 1), last=True)
                t = At(ph, PAIRS - 1)
                weave(iter(()), lane([part("normalise", side.normalise, t, 1, last=True),
                                      part("post", side.post, t, last=True)]))

        block = es.enter_context(nc.Block())

        @block.sync
        def _(sp):
            cr = a["ctx_768"].rearrange("(i b) (p c) d -> i b p (c d)", b=2, c=NC)
            cx = a["ctx_768"].rearrange("(i b) k d -> i b k d", b=2)
            xv = a["x"].rearrange("(i b) t d -> i b t d", b=2)
            ov = out.rearrange("(i b) t d -> i b t d", b=2)

            def one(ap):
                return ap.rearrange("o p n -> (o p) n")

            def load_weights(ph):
                for dst, src in first_loads(ph):
                    sp.dma_start(dst, src).then_inc(f_loaded, 16)
                with nc.allow_non_contiguous_dma(reason="gains and biases as columns, 640 B to 5 KB once a phase"):
                    for dst, src in other_loads(ph):
                        sp.dma_start(dst, src).then_inc(w_loaded, 16)

            def load_x(t):
                i = bass.ds(t.it, 1)
                sp.wait_ge(*got("x_taken", t, 0))
                if t.ph < 2:
                    sp.wait_ge(*got("cst_ready", t, 0))
                if t.ph == 0:
                    for b in range(2):
                        sp.dma_start(x_in[S * b:S * b + T, :], one(xv[i, b, :, :]))\
                            .then_inc(sg["x_loaded"].sem, 16)
                        sp.dma_start(x_in[S * b + T:S * b + S, :], one(xv[i, b, T - 8:T, :]))\
                            .then_inc(sg["x_loaded"].sem, 16)
                else:
                    sp.dma_start(x_in[:, :], one(scratch[i, :, :])).then_inc(sg["x_loaded"].sem, 16)
                if t.ph < 2:
                    for b in range(2):
                        for n, k in enumerate((0, KEYS - 16, 16)):
                            sp.dma_start(cs[S * b + 16 * n:S * b + 16 * n + 16, :], one(cx[i, b, k:k + 16, :]))\
                                .then_inc(sg["cs_loaded"].sem, 16)

            def load_context(t, b):
                sp.wait_ge(*got("ctx_lo", t, b))
                sp.wait_ge(*got("ct_psum", t, 3 * b))
                sp.dma_start(ctx_raw[:, :], one(cr[bass.ds(t.it, 1), b, :, :])).then_inc(sg["cr_loaded"].sem, 16)

            def save_x(t):
                sp.wait_ge(*got("xp_ready", t, per("xp_ready", t)))
                i = bass.ds(t.it, 1)
                if t.ph < 2:
                    sp.dma_start(one(scratch[i, :, :]), x_out[:, :]).then_inc(sg["x_saved"].sem, 16)
                else:
                    for b in range(2):
                        sp.dma_start(one(ov[i, b, :, :]), x_out[S * b:S * b + T, :])\
                            .then_inc(sg["x_saved"].sem, 16)

            for ph in range(3):
                def pair(t, first=False, last=False):
                    load_context(t, 1)
                    if not last:
                        load_x(t + 1)
                        load_context(t + 1, 0)
                    if not first:
                        save_x(t + (-1))

                if ph:
                    sp.wait_ge(*sg["x_saved"].end(ph - 1))
                else:
                    sp.sem_inc(sg["x_saved"].sem, 1)
                    sp.wait_ge(consts, N_CONSTS)
                    load_weights(0)
                    load_x(At(0, 0))
                    load_context(At(0, 0), 0)
                if ph == 0:
                    sp.wait_ge(wp_ready, products_before(1))
                    for dst, src in late_loads():
                        sp.dma_start(dst, src).then_inc(l_loaded, 16)
                pair(At(ph, 0), first=True)
                with sp.Fori(1, PAIRS - 1) as it:
                    pair(At(ph, it))
                pair(At(ph, PAIRS - 1), last=True)
                if ph < 2:
                    sp.wait_ge(*sg["xm_ready"].end(ph))
                    load_weights(ph + 1)
                    sp.wait_ge(*got("x_saved", At(ph, 1), 0))
                    load_x(At(ph + 1, 0))
                    load_context(At(ph + 1, 0), 0)
                save_x(At(ph, PAIRS - 1))
            sp.wait_ge(*sg["x_saved"].end(2))

        @block.tensor
        def _(pe):
            mm, tr = nc.tensor.matmul, nc.tensor.transpose

            def both(dst, lhsT, rhs, first=True, last=True):
                for i in range(2):
                    z = mm(dst, lhsT(i), rhs(i), start=(first and i == 0), stop=(last and i == 1))
                return z

            class side(Idle):
                @staticmethod
                def prologue(ph):
                    if ph == 0:
                        pe.sem_inc(sg["ct_psum"].sem, 1)
                        pe.sem_inc(sg["pv_done"].sem, 36)
                        pe.sem_inc(sg["rp_psum"].sem, 1)
                        pe.wait_ge(consts, N_CONSTS)
                    else:
                        pe.wait_ge(*sg["xp_ready"].end(ph - 1))
                    pe.wait_ge(*factors_loaded(ph))
                    fq, fk, fv, fo = factor_views(ph)
                    dh, n0 = DH[ph], products_before(ph)

                    def product(h):
                        f = factorT(ph, h)
                        pe.wait_ge(wt_ready, n0 + h + 1)
                        if n0 + h >= 2:
                            pe.wait_ge(wp_ready, n0 + h - 1)
                        for i in range(2):
                            mm(ps_u[0:HF, 1 + h % 2, DC * i:DC * i + DC], f[:, HF * i:HF * i + HF], f[:, 160:256],
                               start=True, stop=True)
                        mm(ps_u[0:DC, 1 + h % 2, 192:352], f[:, 256:352], fo[:, h, :],
                           start=True, stop=True).then_inc(wp_psum, 1)

                    for h in range(HEADS[ph]):
                        if n0 + h >= 2:
                            pe.wait_ge(wt_ready, n0 + h - 1)
                        for i in range(2):
                            tr(C(0, dh, h % 2, HF * i, HF), fq[:, i, dh * h:dh * h + dh], ident[0:HF, 0:HF])
                        tr(C(0, dh, h % 2, 160, DC), fk[:, dh * h:dh * h + dh], ident[0:DC, 0:DC])
                        tr(C(0, dh, h % 2, 256, DC), fv[:, dh * h:dh * h + dh], ident[0:DC, 0:DC])\
                            .then_inc(wt_psum, 1)
                        if h:
                            product(h - 1)
                    product(HEADS[ph] - 1)
                    pe.wait_ge(wp_ready, products_before(ph + 1))
                    pe.wait_ge(*weights_loaded(ph))

                @staticmethod
                def inputs(t):
                    pe.wait_ge(*got("cs_loaded", t, 96))
                    tr(side_banks(t)(0, DC, 0, 0, 128), cs[:, :], ident[:, :])
                    pe.wait_ge(*got("x_taken", t, 1))
                    for i in range(2):
                        z = tr(side_banks(t)(0, HF, 1, 128 * i, 128), x_mid[:, HF * i:HF * i + HF], ident[:, :])
                    z.then_inc(*sig("in_psum"))

                @staticmethod
                def norm(t, n, bank):
                    pe.wait_ge(*got("xn_ready", t, n + 1))
                    for i in range(2):
                        z = tr(C(0, HF, bank, 128 * i, 128), xn[:, HF * i:HF * i + HF], ident[:, :])
                    z.then_inc(*sig("xn_psum"))

                @staticmethod
                def probs_T(t, n, tiles, bank):
                    pe.wait_ge(*got("p_ready", t, n + 1))
                    for k in range(tiles):
                        z = tr(side_banks(t)(0, 128, bank, 128 * k, 128), sm[:, 128 * k:128 * k + 128], ident[:, :])
                    z.then_inc(*sig("pt_psum"))

                @staticmethod
                def out_slots(t, n, tiles, vb, d, bank):
                    pe.wait_ge(*got("pt_ready", t, n + 1))
                    for b in range(2):
                        for k in range(tiles):
                            z = mm(side_banks(t)(S * b, S, bank, 2 * d * k, 2 * d), pT3[:, k, S * b:S * b + S],
                                   vb[:, b, 2 * k:2 * k + 2, :], start=True, stop=True)
                    z.then_inc(*sig("o_psum"))

                @staticmethod
                def out_T(t, n, m, bank):
                    pe.wait_ge(*got("o_ready", t, n + 1))
                    for i in range(2):
                        z = tr(side_banks(t)(0, HF, bank, 128 * i, 128), oz[:, HF * i:HF * i + HF], ident[:, :])
                    z.then_inc(*sig("ot_psum"))

                @staticmethod
                def project(t, m, w, bias, bank):
                    pe.wait_ge(*got("ot_ready", t, m + 1))
                    r = side_banks(t)(0, 128, bank, 0, D)
                    mm(r, ones[DC:DC + 1, :], rows[t.ph][:, D * bias:D * bias + D], start=True, stop=False)
                    both(r, lambda i: xT[:, i, :, :], lambda i: w[:, i, :], first=False).then_inc(*sig("rm_psum"))

                @staticmethod
                def resume(t):
                    pe.wait_ge(*got("ut_ready", t, -1))

                @staticmethod
                def pre(t, first=False):
                    yield 1
                    if t.ahead:
                        pe.wait_ge(*weights_loaded(t.ph))
                        side.resume(t)
                    elif not first:
                        if t.ph != 1:
                            pe.wait_ge(*got("mr_ready", t, 0))
                        pe.wait_ge(*got("xp_ready", t, -per("xp_ready", t)))
                    if t.ph == 0:
                        yield from side.pre_0(t)
                    elif t.ph == 1:
                        yield from side.pre_1(t)
                    else:
                        yield from side.pre_2(t)

                @staticmethod
                def pre_0(t):
                    yield 1
                    side.inputs(t)
                    yield 2
                    pe.wait_ge(*got("xt_ready", t, 1))
                    pe.wait_ge(*got("cst_ready", t, 1))
                    for o in range(2):
                        both(C(0, HF, 1, 128 * o, 128), lambda i: l0_wq[:, i, HF * o:HF * o + HF],
                             lambda i: xT[:, i, :, :])
                        kk = C(0, HF, 2, 128 * o, 128).rearrange("p (b w s) -> p b w s", b=2, w=2)
                        for w in range(2):
                            mm(kk[:, :, w, :], l0_wk[w][:, HF * o:HF * o + HF], csT[:, :, 32 * w:32 * w + 32],
                               start=True, stop=True)
                    for b in range(2):
                        for par in range(2):
                            for w in range(2):
                                vw = l0_wv[w].rearrange("p (h e d) -> p h e d", e=2, d=20)[:, :, par, :]
                                z = mm(C(S * par + 32 * w, 32, 0, 80 * b, 80), csT[:, b, 32 * w:32 * w + 32],
                                       vw, start=True, stop=True)
                    z.then_inc(*sig("qkv_psum"))
                    yield 4
                    pe.wait_ge(*got("q_ready", t, 1))
                    pe.wait_ge(*got("kb_ready", t, 1))
                    for b in range(2):
                        for o in range(2):
                            z = mm(C(S * b, S, 1, 256 * o, 256), q_small[:, o, b, :], kb0[:, o, b, :, :],
                                   start=True, stop=True)
                    z.then_inc(*sig("s_psum"))
                    yield 8
                    side.probs_T(t, 0, 4, 2)
                    yield 10
                    pe.wait_ge(*got("vb_ready", t, 1))
                    side.out_slots(t, 0, 4, vb0, 20, 0)
                    yield 12
                    side.out_T(t, 0, 0, 1)
                    yield 14
                    side.project(t, 0, l0_wout, 0, 2)
                    yield 16
                    side.resume(t)
                    side.norm(t, 0, 0)
                    for w in range(2):
                        for j in range(10):
                            if j % 5 == 0:
                                yield 18 + 3 * w + j // 5
                            if j == 0:
                                pe.wait_ge(*(got("q_ready", t, 2) if w else got("ht_ready", t, 1)))
                                pe.wait_ge(*late_loaded())
                            z = both(C(0, 128, 0, 128 * j, 128), lambda i: l1_w[w][:, i, 128 * j:128 * j + 128],
                                     lambda i: hT[:, i, :, :])
                        z.then_inc(*sig("qkv_psum"))
                    for b in range(2):
                        yield 24 + b
                        if b == 0:
                            pe.wait_ge(*got("kb_ready", t, 2))
                            pe.wait_ge(*got("kb2_ready", t, 1))
                        for j in range(10):
                            z = mm(C(S * b, S, 0, 128 * j, 128), qo3[:, j, S * b:S * b + S],
                                   kb1[:, b, 2 * j:2 * j + 2, :], start=True, stop=True)
                    z.then_inc(*sig("s_psum"))
                    for b in range(2):
                        yield 27 + 3 * b
                        if b == 0:
                            pe.wait_ge(*got("s_sub", t, 2))
                        else:
                            pe.wait_ge(*got("vb_ready", t, 2))
                            pe.wait_ge(*got("vb2_ready", t, 1))
                        for par in range(2):
                            for f in range(2):
                                vw = l1_w[2].rearrange("p a (h e d) -> p a h e d", e=2, d=64)
                                z = both(C(S * par, S, f, 0, 320), lambda i: hT[:, i, b, :],
                                         lambda i: vw[:, i, 5 * f:5 * f + 5, par, :])
                        z.then_inc(*sig("qkv_psum"))
                    yield 32
                    pe.wait_ge(*got("vb_ready", t, 3))
                    pe.wait_ge(*got("vb2_ready", t, 2))
                    side.probs_T(t, 1, 10, 0)
                    for b in range(2):
                        yield 34 + b
                        if b == 0:
                            pe.wait_ge(*got("pt_ready", t, 2))
                        for k in range(10):
                            z = mm(C(0, 128, 0, 128 * k + S * b, S), kb1[:, b, 2 * k:2 * k + 2, :],
                                   pT3[:, k, S * b:S * b + S], start=True, stop=True)
                    z.then_inc(*sig("o_psum"))
                    yield 37
                    pe.wait_ge(*got("o_ready", t, 2))
                    r = C(0, 128, 0, 0, D)
                    mm(r, ones[DC:DC + 1, :], rows[t.ph][:, D:2 * D], start=True, stop=False)
                    for j in range(10):
                        z = mm(r, qo3[:, j, :], l1_wo[:, j, :], start=False, stop=(j == 9))
                    z.then_inc(*sig("rm_psum"))
                    yield 39
                    side.norm(t, 1, 1)

                @staticmethod
                def pre_1(t):
                    yield 1
                    side.inputs(t)
                    yield 2
                    pe.wait_ge(*got("xt_ready", t, 1))
                    pe.wait_ge(*got("cst_ready", t, 1))
                    for b in range(2):
                        mm(side_banks(t)(0, NCA, 0, S * b, S), csT[:, b, 28:32], selc[:, :], start=True, stop=True)
                    for b in range(2):
                        for par in range(2):
                            z = mm(side_banks(t)(S * par, S, 2, 80 * b, 80), ident[:, S * b:S * b + S],
                                   x_mid[:, :].rearrange("p (h e d) -> p h e d", e=2, d=20)[:, :, par, :],
                                   start=True, stop=True)
                    z.then_inc(*sig("qkv_psum"))
                    yield 4
                    pe.wait_ge(*got("ca_ready", t, 1))
                    for o in range(2):
                        z = mm(side_banks(t)(0, HF, 1, 128 * o, 128), l2_wqca[:, HF * o:HF * o + HF], caS[:, :],
                               start=True, stop=True)
                    z.then_inc(*sig("ca_psum"))
                    yield 6
                    pe.wait_ge(*got("q_ready", t, 1))
                    pe.wait_ge(*got("kb_ready", t, 1))
                    for b in range(2):
                        for o in range(2):
                            z = mm(side_banks(t)(S * b, S, 0, 256 * o, 256), q_small[:, o, b, :], kb2[:, o, b, :, :],
                                   start=True, stop=True)
                    z.then_inc(*sig("s_psum"))
                    yield 10
                    pe.wait_ge(*got("vb_ready", t, 1))
                    side.probs_T(t, 0, 4, 2)
                    yield 12
                    side.out_slots(t, 0, 4, vb0, 20, 1)
                    yield 14
                    side.out_T(t, 0, 0, 0)
                    yield 16
                    pe.wait_ge(*got("ot_ready", t, 1))
                    for o in range(2):
                        both(side_banks(t)(0, HF, 1, 128 * o, 128), lambda i: l0_wq[:, i, HF * o:HF * o + HF],
                             lambda i: xT[:, i, :, :])
                        mm(side_banks(t)(0, HF, 2, 8 * o, 8), l2_wkca[:, HF * o:HF * o + HF], csT[:, :, 28:32],
                           start=True, stop=True)
                    for b in range(2):
                        z = mm(side_banks(t)(0, 32, 0, D * b, D), ca_r[:, b, :, :].rearrange("p h k -> p (h k)"),
                               l2_wvca, start=True, stop=True)
                    z.then_inc(*sig("ca_psum"))
                    yield 18
                    pe.wait_ge(*got("q_ready", t, 2))
                    pe.wait_ge(*got("k2_ready", t, 1))
                    for b in range(2):
                        for o in range(2):
                            z = mm(side_banks(t)(S * b, S, 2, 16 * o, 16), q_small[:, o, b, :], k2b[:, o, b, :],
                                   start=True, stop=True)
                    z.then_inc(*sig("s_psum"))
                    yield 22
                    pe.wait_ge(*got("p_ready", t, 2))
                    tr(side_banks(t)(0, 32, 0, 0, 128), p2[:, :], ident[:, :]).then_inc(*sig("pt_psum"))
                    yield 24
                    pe.wait_ge(*got("pt_ready", t, 2))
                    for b in range(2):
                        z = mm(side_banks(t)(S * b, S, 1, 0, D), pT[0:32, S * b:S * b + S], v2b[:, b, :], start=True, stop=True)
                    z.then_inc(*sig("o_psum"))
                    yield 26
                    side.out_T(t, 1, 1, 0)
                    yield 28
                    side.project(t, 1, l0_wout, 0, 1)

                @staticmethod
                def pre_2(t):
                    yield 2
                    side.norm(t, 0, 0)
                    yield 4
                    side.resume(t)
                    pe.wait_ge(*got("ht_ready", t, 1))
                    for o in range(2):
                        for w in range(2):
                            both(C(0, HF, 1 + w, 128 * o, 128), lambda i: l3_w[w][:, i, HF * o:HF * o + HF],
                                 lambda i: hT[:, i, :, :])
                    for b in range(2):
                        for par in range(2):
                            vw = l3_w[2].rearrange("p a (h e d) -> p a h e d", e=2, d=8)
                            z = both(C(S * par, S, 0, 80 * b, 80), lambda i: hT[:, i, b, :],
                                     lambda i: vw[:, i, :, par, :])
                    z.then_inc(*sig("qkv_psum"))
                    yield 7
                    pe.wait_ge(*got("q_ready", t, 1))
                    pe.wait_ge(*got("kb_ready", t, 1))
                    pe.wait_ge(*got("vb_ready", t, 1))
                    for b in range(2):
                        for o, h0, h1 in ((0, 0, 8), (0, 8, 10), (1, 0, 6), (1, 6, 10)):
                            z = mm(C(S * b, S, 0, 640 * o + S * h0, S * (h1 - h0)), q_small[:, o, b, :],
                                   kb3[:, o, b, h0:h1, :], start=True, stop=True)
                    z.then_inc(*sig("s_psum"))
                    yield 11
                    side.probs_T(t, 0, 10, 0)
                    yield 13
                    side.out_slots(t, 0, 10, vb3, 8, 0)
                    yield 15
                    side.out_T(t, 0, 0, 1)
                    yield 17
                    side.project(t, 0, l3_o, 0, 2)
                    yield 19
                    side.norm(t, 1, 0)

                @staticmethod
                def queries(t, b):
                    for g, (h0, n) in enumerate(t.groups):
                        yield 1 + g
                        if g == 0:
                            pe.wait_ge(*(got("mr_ready", t, 1) if b else got("xm_ready", t, per("xm_ready", t))))
                            if t.ph != 1:
                                pe.wait_ge(*got("ht_ready", t, 2))
                            elif b == 0:
                                side.resume(t)
                        for h in range(n):
                            z = both(C(0, DC, g, S * h, S), lambda i: w_m[:, i, DC * (h0 + h):DC * (h0 + h) + DC],
                                     lambda i: hT[:, i, b, :])
                        z.then_inc(*sig("qt_psum"))

                @staticmethod
                def context(t, b):
                    for r in range(NPIECE):
                        yield 1 + r
                        if r == 0:
                            pe.wait_ge(*got("cr_loaded", t, 16 * (b + 1)))
                            pe.wait_ge(*got("ql_ready", t, len(t.groups) * (b + 1)))
                            if b:
                                pe.wait_ge(*got("ut_ready", t, 0))
                        if r >= banks(t):
                            pe.wait_ge(*got("ctl_ready", t, NPIECE * b + r - banks(t) + 1))
                        for j in range(4):
                            c = 4 * r + j
                            z = tr(C(0, DC, r % banks(t), KP * j, KP), ctx_raw[:, DC * c:DC * c + DC], ident[0:KP, 0:KP])
                        z.then_inc(*sig("ct_psum"))

                @staticmethod
                def maxima(t, b):
                    tiles = t.heads // 2
                    for k in range(tiles):
                        for r in range(NPIECE):
                            n = NPIECE * k + r
                            yield 1 + n
                            if n == 0:
                                pe.wait_ge(*got("ctl_ready", t, NPIECE * (b + 1)))
                            if n >= banks(t):
                                pe.wait_ge(*got("mp_ready", t, NPIECE * tiles * b + n - banks(t) + 1))
                            mm(C(0, 112, n % banks(t), 0, PIECE), q_hi[0:DC, b, 112 * k:112 * k + 112],
                               ctxT_hi[0:DC, b, PIECE * r:PIECE * r + PIECE], start=True, stop=True)\
                                .then_inc(*sig("mp_psum"))
                    yield 3 * tiles + 3
                    pe.wait_ge(*got("mx_ready", t, b + 1))
                    for k in range(tiles):
                        z = mm(C(DC, 1, k // 4, 112 * (k % 4), 112), mx[:, k:k + 1], ident[0:112, 0:112],
                               start=True, stop=True)
                    z.then_inc(*sig("mr_psum"))

                @staticmethod
                def normalise(t, b, last=False):
                    yield 1
                    pe.wait_ge(*got("u_copied", t, len(t.groups) * (b + 1)))
                    if b == 0:
                        pe.wait_ge(*got("mr_ready", t, 2))
                        pe.wait_ge(*got("xp_ready", t, 0))
                        if not last and t.ph != 1:
                            pe.wait_ge(*(got("ht_ready", t + 1, 1) if t.ph else got("xm_ready", t + 1, 1)))
                    else:
                        pe.wait_ge(*(got("ut_ready", t, 1) if last else got("ql_ready", t + 1, 2 * len(t.groups))))
                    for k in range(t.heads // 2):
                        z = mm(C(0, 112, 0, k, 1), u_sb[DC:DC + 1, 112 * k:112 * k + 112], ones[DC:DC + 1, 0:1],
                               start=True, stop=True)
                    z.then_inc(*sig("sum_psum"))
                    yield 4
                    pe.wait_ge(*got("diag_ready", t, b + 1))
                    for g, (h0, n) in enumerate(t.groups):
                        z = mm(C(0, DC, g, 0, T * n), ones[0:112, 0:DC], diags[t.ph][:, T * h0:T * (h0 + n)],
                               start=True, stop=True)
                    z.then_inc(*sig("rb_psum"))

                @staticmethod
                def post(t, last=False):
                    yield 1
                    pe.wait_ge(*got("ut_ready", t, 2))
                    if not last and t.ph != 1:
                        pe.wait_ge(*got("mr_ready", t, 4))
                    r = side_banks(t)(0, 128, 0, 0, D)
                    if t.ph != 1:
                        mm(r, ones[DC:DC + 1, :], rows[t.ph][:, D * (2 - t.ph // 2):D * (3 - t.ph // 2)], start=True, stop=False)
                    for h in range(t.heads):
                        z = mm(r, uT[:, h, :, :], w_n[:, h, :], start=(t.ph == 1 and h == 0), stop=(h == t.heads - 1))
                    z.then_inc(*sig("rp_psum"))
                    if t.ph == 1:
                        return
                    yield 6
                    pe.wait_ge(*got("xnf_ready", t, 1))
                    for i in range(2):
                        z = tr(C(0, HF, 1, 128 * i, 128), xnF[:, HF * i:HF * i + HF], ident[:, :])
                    z.then_inc(*sig("xnf_psum"))
                    for c in range(10):
                        if c % 5 == 0:
                            yield 8 + c // 5
                        if c == 0:
                            pe.wait_ge(*got("hf_ready", t, 1))
                        z = both(FC(c), lambda i: fw1[:, i, 128 * c:128 * c + 128], lambda i: hF[:, i, :, :])
                    z.then_inc(*sig("f_psum"))
                    yield 14
                    pe.wait_ge(*got("ff_ready", t, 1))
                    mm(r, ones[DC:DC + 1, :], rows[t.ph][:, D * (3 - t.ph // 2):D * (4 - t.ph // 2)], start=True, stop=False)
                    for c in range(5):
                        z = mm(r, gT[:, c, :], fw2[:, c, :], start=False, stop=(c == 4))
                    z.then_inc(*sig("rp_psum"))

            def main(t, b, first=False, last=False):
                G = t.groups
                total = NC * len(G)
                before = total * b

                def scores(n):
                    c, g = divmod(n, len(G))
                    h0, nh = G[g]
                    kp = KP if c < 8 or t.ph != 1 else KP - 1
                    q = slice(T * h0, T * (h0 + nh))
                    k = slice(KP * c, KP * c + kp)
                    dst = ps_s[0:kp, (before + n) % 2, 0:T * nh]
                    pe.wait_ge(*got("exp_done", t, before + n - 1))
                    mm(dst, ctxT_hi[:, b, k], q_hi[:, b, q], start=True, stop=False)
                    mm(dst, ctxT_hi[0:DC, b, k], q_lo[:, b, q], start=False, stop=False)
                    mm(dst, ctxT_lo[:, b, k], q_hi[0:DC, b, q], start=False, stop=True).then_inc(*sig("sc_psum"))

                def outputs(n):
                    c, g = divmod(n % total, len(G))
                    cb = b if n >= 0 else 1 - b
                    kp = KP if c < 8 or t.ph != 1 else KP - 1
                    w, s = T * G[g][1], (before + n) % 3
                    pe.wait_ge(*got("pl_ready", t, before + n + 1))
                    if c == 0:
                        pe.wait_ge(*got("u_copied", t, len(G) * (b - 1) + g + 1))
                    dst = ps_u[0:DC + 1, g, 0:w]
                    mm(dst, ctx_hi[0:kp, cb, c, :], p_hi[0:kp, s, 0:w], start=(c == 0), stop=False)
                    mm(ps_u[0:DC, g, 0:w], ctx_lo[0:kp, cb, c, :], p_hi[0:kp, s, 0:w], start=False, stop=False)
                    mm(dst, ctx_hi[0:kp, cb, c, :], p_lo[0:kp, s, 0:w],
                       start=False, stop=(c == NC - 1)).then_inc(*sig("pv_done"))

                for n in range(total + 2 if last else total):
                    yield 2 * n
                    if n == 0:
                        pe.wait_ge(*got("mr_ready", t, b + 1))
                        pe.wait_ge(*got("ctx_lo", t, b + 1))
                    if n < total:
                        scores(n)
                    yield 2 * n + 1
                    if n >= 2 or not first:
                        outputs(n - 2)

            schedule(pe, side, main)

        @block.vector
        def _(dve):
            V = nc.vector

            class side(Idle):
                @staticmethod
                def prologue(ph):
                    if ph == 0:
                        for s, n in (("x_taken", 1), ("cst_ready", 1), ("ut_ready", 2), ("x_handed", 1),
                                     ("xp_ready", 1)):
                            dve.sem_inc(sg[s].sem, n)
                        V.memset(ctxT_hi[DC:DC + 1, :, :].bitcast(F32), 1.0).then_inc(consts, 1)
                    dh, n0 = DH[ph], products_before(ph)
                    for h in range(HEADS[ph]):
                        dve.wait_ge(wt_psum, n0 + h + 1)
                        if n0 + h >= 4:
                            dve.wait_ge(wp_psum, n0 + h - 3)
                        V.tensor_copy(factorT(ph, h), C(0, dh, h % 2, 0, 352)).then_inc(wt_ready, 1)
                    dve.wait_ge(*weights_loaded(ph))
                    dve.wait_ge(consts, N_CONSTS + (ph == 2))

                @staticmethod
                def take(t):
                    dve.wait_ge(*got("x_loaded", t, per("x_loaded", t)))
                    dve.wait_ge(*got("x_handed", t, 0))
                    V.tensor_copy(x_mid[:, :], x_in[:, :]).then_inc(*sig("x_taken"))

                @staticmethod
                def add(t, n, bank):
                    dve.wait_ge(*got("rm_psum", t, n + 1))
                    V.tensor_tensor(x_mid[:, :], x_mid[:, :], side_banks(t)(0, 128, bank, 0, D), ALU.add)\
                        .then_inc(*sig("xm_ready"))

                @staticmethod
                def norm(t, n):
                    if n == 0 and t.ph == 2:
                        dve.wait_ge(*got("x_taken", t, 1))
                    else:
                        dve.wait_ge(*got("xm_ready", t, n + (t.ph == 0)))
                    V.bn_stats(stats[:, :], x_mid[:, :]).then_inc(*sig("ln_stats"))
                    dve.wait_ge(*got("ln_stats", t, n + 1))
                    V.tensor_copy(count[:, :], stats[:, 0:1])
                    V.bn_aggr(mv[:, :], stats[:, :]).then_inc(*sig("ln_mean"))
                    dve.wait_ge(*got("ln_rstd", t, n + 1))
                    V.tensor_scalar(xn[:, :], x_mid[:, :], mv[:, 0:1], rstd[:, :], ALU.subtract, ALU.mult)\
                        .then_inc(*sig("xn_ready"))

                @staticmethod
                def softmax(t, n, src, dst, m, s, axes, half=None):
                    dve.wait_ge(*got("s_psum", t, n + 1))
                    V.tensor_reduce(m, src, AX.X, ALU.max).then_inc(*sig("s_max"))
                    dve.wait_ge(*got("s_max", t, n + 1))
                    V.tensor_tensor(dst, src, m.unsqueeze(axes).broadcast_to(dst.shape), ALU.subtract)\
                        .then_inc(*sig("s_sub"))
                    yield
                    dve.wait_ge(*got("s_exp", t, n + 1))
                    V.tensor_reduce(s, dst, AX.X, ALU.add).then_inc(*sig("s_sum"))
                    dve.wait_ge(*got("s_sum", t, n + 1))
                    V.reciprocal(s, s).then_inc(*sig("s_rec"))
                    k = n + 1 if t.ph else 2 * n + 1
                    dve.wait_ge(*got("s_rec", t, k))
                    if half is not None:
                        V.tensor_scalar(half, half, 0.5, None, ALU.mult).then_inc(*sig("s_rec"))
                        dve.wait_ge(*got("s_rec", t, k + 1))
                    V.tensor_tensor(dst, dst, s.unsqueeze(axes).broadcast_to(dst.shape), ALU.mult)\
                        .then_inc(*sig("p_ready"))
                    yield

                @staticmethod
                def v_blocks(t, vb, bank):
                    for par in range(2):
                        r = slice(S * par, S * par + S)
                        z = V.tensor_copy(vb[r, :, par::2, :], side_banks(t)(S * par, S, bank, 0, 160)
                                          .rearrange("p (b h d) -> p b h d", b=2, h=vb.shape[2] // 2))
                    z.then_inc(*sig("vb_ready"))

                @staticmethod
                def pre(t, first=False):
                    if t.ahead:
                        yield 1
                        dve.wait_ge(consts, N_CONSTS + (t.ph == 2))
                    if t.ph == 0:
                        yield from side.pre_0(t)
                    elif t.ph == 1:
                        yield from side.pre_1(t)
                    else:
                        yield from side.pre_2(t)

                @staticmethod
                def pre_0(t):
                    yield 1
                    side.take(t)
                    dve.wait_ge(*got("in_psum", t, 1))
                    V.tensor_copy(csT[:, :, :], C(0, DC, 0, 0, 128).rearrange("p (b s) -> p b s", b=2))\
                        .then_inc(*sig("cst_ready"))
                    yield 3
                    dve.wait_ge(*got("qkv_psum", t, 1))
                    for o in range(2):
                        kk = C(0, HF, 2, 128 * o, 128).rearrange("p (b s) -> p b s", b=2).unsqueeze(2)
                        z = V.tensor_tensor(kb0[:, o, :, :, :], kk.broadcast_to([HF, 2, 4, S]),
                                            hm[:, 0:4].unsqueeze(1).unsqueeze(3).broadcast_to([HF, 2, 4, S]), ALU.mult)
                    z.then_inc(*sig("kb_ready"))
                    side.v_blocks(t, vb0, 0)
                    yield 5
                    s = C(0, 128, 1, 0, 512).rearrange("p (h g w) -> p h g w", h=8, g=4)[:, :, 0:3, :]
                    p = sm[:, 0:512].rearrange("p (h g w) -> p h g w", h=8, g=4)[:, :, 0:3, :]
                    m3, s3 = (v[:, :].rearrange("p (h g) -> p h g", g=3) for v in (smx, ssum))
                    x = side.softmax(t, 0, s, p, m3, s3, 3, half=s3[:, :, 0:3:2])
                    next(x)
                    yield 7
                    next(x)
                    yield 11
                    dve.wait_ge(*got("o_psum", t, 1))
                    V.tensor_copy(oz[:, :], C(0, 128, 0, 0, D)).then_inc(*sig("o_ready"))
                    yield 15
                    side.add(t, 0, 2)
                    side.norm(t, 0)
                    yield 23
                    dve.wait_ge(*got("qkv_psum", t, 3))
                    V.tensor_copy(kb1[S:2 * S, :, 1::2, :].rearrange("p b j s -> p j b s"),
                                  C(S, S, 0, 0, 1280).rearrange("p (j b s) -> p j b s", j=10, b=2))\
                        .then_inc(*sig("kb_ready"))
                    yield 26
                    s = C(0, 128, 0, 0, 1280).rearrange("p (h w) -> p h w", h=20)[:, :, 0:T]
                    x = side.softmax(t, 1, s, smv[:, :, 0:T], smx[:, 0:20], ssum[:, 0:20], 2)
                    next(x)
                    yield 28
                    next(x)
                    for b in range(2):
                        yield 29 + 2 * b
                        dve.wait_ge(*got("qkv_psum", t, 4 + b))
                        V.tensor_copy(kb1[S:2 * S, b, 1::2, :].rearrange("p (f e) d -> p f e d", f=2),
                                      C(S, S, 0, 0, 1024).rearrange("p (f n) -> p f n", f=2)[:, :, 0:320]
                                      .rearrange("p f (e d) -> p f e d", e=5)).then_inc(*sig("vb_ready"))
                    yield 36
                    dve.wait_ge(*got("o_psum", t, 2))
                    V.tensor_copy(qo[:, :], C(0, 128, 0, 0, 1280)).then_inc(*sig("o_ready"))
                    yield 38
                    side.add(t, 1, 0)
                    side.norm(t, 1)

                @staticmethod
                def pre_1(t):
                    yield 1
                    side.take(t)
                    dve.wait_ge(*got("in_psum", t, 1))
                    V.tensor_copy(csT[:, :, :], side_banks(t)(0, DC, 0, 0, 128).rearrange("p (b s) -> p b s", b=2))\
                        .then_inc(*sig("cst_ready"))
                    yield 3
                    dve.wait_ge(*got("qkv_psum", t, 1))
                    V.tensor_copy(caS[:, :], side_banks(t)(0, NCA, 0, 0, 128)).then_inc(*sig("ca_ready"))
                    dve.wait_ge(*got("cst_ready", t, 1))
                    V.tensor_copy(ca_r[:, :, :, :], csT[:, :, 28:32].unsqueeze(2).broadcast_to([DC, 2, 8, NCA]))
                    side.v_blocks(t, vb0, 2)
                    dve.wait_ge(*got("xt_ready", t, 1))
                    for o in range(2):
                        z = V.tensor_tensor(kb2[:, o, :, :, :], hT[:, o, :, :].unsqueeze(2).broadcast_to([HF, 2, 4, S]),
                                            hm[:, 0:4].unsqueeze(1).unsqueeze(3).broadcast_to([HF, 2, 4, S]), ALU.mult)
                    z.then_inc(*sig("kb_ready"))
                    yield 7
                    s = side_banks(t)(0, 128, 0, 0, 512).rearrange("p (h w) -> p h w", h=8)[:, :, 0:T]
                    x = side.softmax(t, 0, s, smv[:, 0:8, 0:T], smx[:, 0:8], ssum[:, 0:8], 2)
                    next(x)
                    yield 9
                    next(x)
                    yield 13
                    dve.wait_ge(*got("o_psum", t, 1))
                    V.tensor_copy(oz[:, :], side_banks(t)(0, 128, 1, 0, D)).then_inc(*sig("o_ready"))
                    yield 17
                    dve.wait_ge(*got("ca_psum", t, 2))
                    for b in range(2):
                        V.tensor_tensor(k2b[:, :, b, :].rearrange("p o (h k) -> p o h k", k=NCA),
                                        side_banks(t)(0, HF, 2, 0, 16).rearrange("p (o b k) -> p o b k", o=2, b=2)[:, :, b, :]
                                        .unsqueeze(2).broadcast_to([HF, 2, 4, NCA]),
                                        hm[:, 0:4].unsqueeze(1).unsqueeze(3).broadcast_to([HF, 2, 4, NCA]), ALU.mult)
                    V.tensor_tensor(v2b[:, :, :], side_banks(t)(0, 32, 0, 0, 320).rearrange("p (b n) -> p b n", b=2),
                                    hm32[:, :].unsqueeze(1).broadcast_to([32, 2, D]), ALU.mult)\
                        .then_inc(*sig("k2_ready"))
                    yield 19
                    s = side_banks(t)(0, 128, 2, 0, 32).rearrange("p (h w) -> p h w", h=8)
                    x = side.softmax(t, 1, s, p2[:, :].rearrange("p (h w) -> p h w", h=8),
                                     smx[:, 0:8], ssum[:, 0:8], 2)
                    next(x)
                    yield 21
                    next(x)
                    yield 25
                    dve.wait_ge(*got("o_psum", t, 2))
                    V.tensor_copy(oz[:, :], side_banks(t)(0, 128, 1, 0, D)).then_inc(*sig("o_ready"))
                    yield 29
                    side.add(t, 0, 1)

                @staticmethod
                def pre_2(t):
                    yield 1
                    side.take(t)
                    side.norm(t, 0)
                    yield 5
                    dve.wait_ge(*got("qkv_psum", t, 1))
                    for o in range(2):
                        for b in range(2):
                            z = V.tensor_tensor(kb3[:, o, b, :, :],
                                                C(0, HF, 2, 128 * o + S * b, S).unsqueeze(1).broadcast_to([HF, 10, S]),
                                                hm[:, 4:14].unsqueeze(2).broadcast_to([HF, 10, S]), ALU.mult)
                    z.then_inc(*sig("kb_ready"))
                    side.v_blocks(t, vb3, 0)
                    yield 8
                    s = C(0, 128, 0, 0, 1280).rearrange("p (h w) -> p h w", h=20)[:, :, 0:T]
                    x = side.softmax(t, 0, s, smv[:, :, 0:T], smx[:, 0:20], ssum[:, 0:20], 2)
                    next(x)
                    yield 10
                    next(x)
                    yield 14
                    dve.wait_ge(*got("o_psum", t, 1))
                    V.tensor_copy(oz[:, :], C(0, 128, 0, 0, D)).then_inc(*sig("o_ready"))
                    yield 18
                    side.add(t, 0, 2)
                    side.norm(t, 1)

                @staticmethod
                def queries(t, b):
                    for g, (h0, n) in enumerate(t.groups):
                        yield 2 + g
                        k = len(t.groups) * b + g + 1
                        dve.wait_ge(*got("qh_ready", t, k))
                        q = slice(T * h0, T * (h0 + n))
                        V.tensor_tensor(q_lo[:, b, q].rearrange("p (h s) -> p h s", h=n),
                                        C(0, DC, g, 0, S * n).rearrange("p (h s) -> p h s", h=n)[:, :, 0:T],
                                        q_hi[0:DC, b, q].bitcast(F32).rearrange("p (h s) -> p h s", h=n),
                                        ALU.subtract).then_inc(*sig("ql_ready"))

                @staticmethod
                def context(t, b):
                    yield 1
                    dve.wait_ge(*got("cr_loaded", t, 16 * (b + 1)))
                    V.tensor_copy(ctx_hi[:, b, :, 0:DC], ctx_raw[:, :].rearrange("p (c d) -> p c d", c=NC))\
                        .then_inc(*sig("ctx_hi"))
                    for r in range(NPIECE):
                        yield 2 + r
                        dve.wait_ge(*got("cth_ready", t, NPIECE * b + r + 1))
                        k = slice(PIECE * r, PIECE * r + PIECE)
                        V.tensor_tensor(ctxT_lo[:, b, k], C(0, DC, r % banks(t), 0, PIECE), ctxT_hi[0:DC, b, k].bitcast(F32),
                                        ALU.subtract).then_inc(*sig("ctl_ready"))

                @staticmethod
                def maxima(t, b):
                    tiles = t.heads // 2
                    for k in range(tiles):
                        for r in range(NPIECE):
                            n = NPIECE * k + r
                            yield 2 + n
                            dve.wait_ge(*got("mp_psum", t, NPIECE * tiles * b + n + 1))
                            if t.ph == 1 and r == NPIECE - 1:
                                z = V.tensor_reduce(mpiece[:, k, r:r + 1], C(0, 112, n % banks(t), 0, PIECE)
                                                    .rearrange("p (c s) -> p c s", c=4)[:, :, 0:KP - 1], AX.XY, ALU.max)
                            else:
                                z = V.tensor_reduce(mpiece[:, k, r:r + 1], C(0, 112, n % banks(t), 0, PIECE), AX.X, ALU.max)
                            z.then_inc(*sig("mp_ready"))
                    yield 3 * tiles + 2
                    dve.wait_ge(*got("mp_ready", t, NPIECE * tiles * (b + 1)))
                    V.tensor_reduce(mx[:, 0:tiles], mpiece[:, 0:tiles, :], AX.X, ALU.max).then_inc(*sig("mx_ready"))

                @staticmethod
                def normalise(t, b, last=False):
                    yield 2
                    tiles = t.heads // 2
                    dve.wait_ge(*got("sum_psum", t, b + 1))
                    V.reciprocal(srec[:, 0:tiles], C(0, 112, 0, 0, tiles)).then_inc(*sig("rec_ready"))
                    dve.wait_ge(*got("rec_ready", t, b + 1))
                    V.tensor_tensor(diags[t.ph][:, 0:112 * tiles].rearrange("p (k q) -> p k q", q=112),
                                    ident[0:112, 0:112].unsqueeze(1).broadcast_to([112, tiles, 112]),
                                    srec[:, 0:tiles].unsqueeze(2).broadcast_to([112, tiles, 112]), ALU.mult)\
                        .then_inc(*sig("diag_ready"))
                    for g, (h0, n) in enumerate(t.groups):
                        yield 5 + g
                        if g == 0:
                            dve.wait_ge(*got("rb_psum", t, b + 1))
                            dve.wait_ge(*got("rp_psum", t, 0))
                        z = V.tensor_tensor(uT[:, h0:h0 + n, b, 0:T],
                                            u_sb[0:DC, T * h0:T * (h0 + n)].rearrange("p (h s) -> p h s", h=n),
                                            C(0, DC, g, 0, T * n).rearrange("p (h s) -> p h s", h=n), ALU.mult)
                    z.then_inc(*sig("ut_ready"))

                @staticmethod
                def hand(t):
                    yield 1
                    dve.wait_ge(*got("xp_ready", t, 0))
                    dve.wait_ge(*got("xm_ready", t, per("xm_ready", t)))
                    V.tensor_copy(x_post[:, :], x_mid[:, :]).then_inc(*sig("x_handed"))

                @staticmethod
                def add_post(t, n):
                    dve.wait_ge(*got("rp_psum", t, n + 1))
                    if n == 0:
                        dve.wait_ge(*got("x_handed", t, 1))
                    final = n + 1 == per("xp_ready", t)
                    if final:
                        dve.wait_ge(*got("x_saved", t, 0))
                    V.tensor_tensor((x_out if final else x_post)[:, :], x_post[:, :], side_banks(t)(0, 128, 0, 0, D), ALU.add)\
                        .then_inc(*sig("xp_ready"))

                @staticmethod
                def post(t, last=False):
                    yield 2
                    side.add_post(t, 0)
                    if t.ph == 1:
                        return
                    dve.wait_ge(*got("xp_ready", t, 1))
                    V.bn_stats(statsF[:, :], x_post[:, :]).then_inc(*sig("lnf_stats"))
                    dve.wait_ge(*got("lnf_stats", t, 1))
                    V.tensor_copy(countF[:, :], statsF[:, 0:1])
                    V.bn_aggr(mvF[:, :], statsF[:, :]).then_inc(*sig("lnf_mean"))
                    yield 4
                    dve.wait_ge(*got("lnf_rstd", t, 1))
                    V.tensor_scalar(xnF[:, :], x_post[:, :], mvF[:, 0:1], rstdF[:, :], ALU.subtract, ALU.mult)\
                        .then_inc(*sig("xnf_ready"))
                    yield 12
                    dve.wait_ge(*got("gelu_ready", t, 1))
                    for c in range(5):
                        z = V.scalar_tensor_tensor(gT[:, c, :], FC(c), bff[:, c:c + 1], gT[:, c, :], ALU.add, ALU.mult)
                    z.then_inc(*sig("ff_ready"))
                    yield 15
                    side.add_post(t, 1)

            def main(t, b, first=False, last=False):
                return iter(())

            schedule(dve, side, main)

        @block.gpsimd
        def _(pool):
            P = nc.gpsimd
            for tile, v in ((ident, 0.0), (ones, 1.0), (neghalf, -0.5), (eps, EPS), (sm, 0.0), (kvb, 0.0), (vb_s, 0.0), (cs, 0.0),
                            (uT, 0.0)):
                P.memset(tile[tuple(slice(None) for _ in tile.shape)], v).then_inc(consts, 1)
            P.memset(ctx_hi[:, :, :, DC:DC + 1].bitcast(F32), 1.0).then_inc(consts, 1)
            pool.wait_ge(consts, N_CONSTS - 1)
            P.affine_select(out=ident[:, :], in_=ident[:, :], compare_op=ALU.not_equal, fill=1.0,
                            base=0, pattern=[[-1, 128]], channel_multiplier=1).then_inc(consts, 1)

            def rsqrt(t, n, mean, var, out_, names):
                m, v, r = names
                pool.wait_ge(*got(m, t, n + 1))
                P.tensor_tensor(var[:, :], mean[:, 1:2], eps[:, :], ALU.add).then_inc(*sig(v))
                pool.wait_ge(*got(v, t, n + 1))
                P.tensor_tensor(out_[:, :], var[:, :], neghalf[:, :], ALU.pow).then_inc(*sig(r))

            class side(Idle):
                @staticmethod
                def prologue(ph):
                    if ph == 0:
                        pool.sem_inc(sg["ctx_lo"].sem, 1)
                        pool.sem_inc(sg["pl_ready"].sem, 2)

                @staticmethod
                def pre(t, first=False):
                    names = ("ln_mean", "ln_var", "ln_rstd")
                    if t.ph == 0:
                        yield 15
                        rsqrt(t, 0, mv, ve, rstd, names)
                        yield 38
                        rsqrt(t, 1, mv, ve, rstd, names)
                    if t.ph == 2:
                        yield 1
                        if t.ahead:
                            pool.wait_ge(*sg["xm_ready"].end(1))
                            P.memset(vb_s[:, :], 0.0).then_inc(consts, 1)
                        rsqrt(t, 0, mv, ve, rstd, names)
                        yield 18
                        rsqrt(t, 1, mv, ve, rstd, names)

                @staticmethod
                def context(t, b):
                    yield 2
                    pool.wait_ge(*got("ctx_hi", t, b + 1))
                    P.tensor_tensor(ctx_lo[:, b, :, :], ctx_raw[:, :].rearrange("p (c d) -> p c d", c=NC),
                                    ctx_hi[:, b, :, 0:DC].bitcast(F32), ALU.subtract).then_inc(*sig("ctx_lo"))

                @staticmethod
                def post(t, last=False):
                    if t.ph != 1:
                        yield 2
                        rsqrt(t, 0, mvF, veF, rstdF, ("lnf_mean", "lnf_var", "lnf_rstd"))

            def main(t, b, first=False, last=False):
                G = t.groups
                for n in range(NC * len(G)):
                    yield 2 * n + 2
                    c, g = divmod(n, len(G))
                    kp = KP if c < 8 or t.ph != 1 else KP - 1
                    w, k = T * G[g][1], NC * len(G) * b + n
                    pool.wait_ge(*got("exp_done", t, k + 1))
                    pool.wait_ge(*got("pv_done", t, k - 2))
                    P.tensor_tensor(p_lo[0:kp, k % 3, 0:w], p32[0:kp, k % 2, 0:w],
                                    p_hi[0:kp, k % 3, 0:w].bitcast(F32), ALU.subtract).then_inc(*sig("pl_ready"))

            schedule(pool, side, main)

        @block.scalar
        def _(act):
            A = nc.scalar.activation
            SHORT_SCALE = ((20 ** -0.5, 64 ** -0.5), (20 ** -0.5, 20 ** -0.5), (8 ** -0.5,))

            class side(Idle):
                @staticmethod
                def prologue(ph):
                    if ph == 0:
                        act.sem_inc(sg["exp_done"].sem, 2)
                        act.sem_inc(sg["u_copied"].sem, 3)
                    n0 = products_before(ph)
                    for h in range(HEADS[ph]):
                        act.wait_ge(wp_psum, n0 + h + 1)
                        A(w_m[:, :, DC * h:DC * h + DC],
                          ps_u[0:HF, 1 + h % 2, 0:2 * DC].rearrange("p (a n) -> p a n", a=2), ACT.Copy)
                        A(w_n[:, h, :], ps_u[0:DC, 1 + h % 2, 192:352], ACT.Copy).then_inc(wp_ready, 1)
                    act.wait_ge(*weights_loaded(ph))

                @staticmethod
                def norm(t, n, bank):
                    act.wait_ge(*got("xn_psum", t, n + 1))
                    for i in range(2):
                        z = A(hT[:, i, :, :], C(0, HF, bank, 128 * i, 128).rearrange("p (b s) -> p b s", b=2),
                              ACT.Identity, scale=gb[:, i, 2 * n:2 * n + 1], bias=gb[:, i, 2 * n + 1:2 * n + 2])
                    z.then_inc(*sig("ht_ready"))

                @staticmethod
                def exps(t, n, p):
                    act.wait_ge(*got("s_sub", t, n + 1))
                    A(p, p, ACT.Exp, scale=SHORT_SCALE[t.ph][n]).then_inc(*sig("s_exp"))

                @staticmethod
                def pre(t, first=False):
                    two = "p (a b s) -> p a b s"
                    if t.ahead:
                        yield 1
                        act.wait_ge(*weights_loaded(t.ph))
                    if t.ph < 2:
                        yield 1
                        act.wait_ge(*got("in_psum", t, 1))
                        A((xT, hT)[t.ph][:, :, :, :], side_banks(t)(0, HF, 1, 0, 256).rearrange(two, a=2, b=2), ACT.Copy)\
                            .then_inc(*sig("xt_ready"))
                    if t.ph == 0:
                        yield 3
                        act.wait_ge(*got("qkv_psum", t, 1))
                        A(q_small[:, :, :, :], side_banks(t)(0, HF, 1, 0, 256).rearrange(two, a=2, b=2), ACT.Copy)\
                            .then_inc(*sig("q_ready"))
                        yield 6
                        side.exps(t, 0, sm[:, 0:512].rearrange("p (h w) -> p h w", h=8)[:, :, 0:48])
                        yield 9
                        act.wait_ge(*got("pt_psum", t, 1))
                        A(pT[:, 0:512], side_banks(t)(0, 128, 2, 0, 512), ACT.Copy).then_inc(*sig("pt_ready"))
                        yield 13
                        act.wait_ge(*got("ot_psum", t, 1))
                        A(xT[:, :, :, :], side_banks(t)(0, HF, 1, 0, 256).rearrange(two, a=2, b=2), ACT.Copy)\
                            .then_inc(*sig("ot_ready"))
                        yield 17
                        side.norm(t, 0, 0)
                        yield 20
                        act.wait_ge(*got("qkv_psum", t, 2))
                        A(qo[:, :], side_banks(t)(0, 128, 0, 0, 1280), ACT.Copy).then_inc(*sig("q_ready"))
                        yield 23
                        act.wait_ge(*got("qkv_psum", t, 3))
                        A(kb1[0:S, :, 0::2, :].rearrange("p b j s -> p j b s"),
                          side_banks(t)(0, S, 0, 0, 1280).rearrange("p (j b s) -> p j b s", j=10, b=2), ACT.Copy)\
                            .then_inc(*sig("kb2_ready"))
                        yield 27
                        side.exps(t, 1, smv[:, :, 0:T])
                        for b in range(2):
                            yield 29 + 2 * b
                            act.wait_ge(*got("qkv_psum", t, 4 + b))
                            A(kb1[0:S, b, 0::2, :].rearrange("p (f e) d -> p f e d", f=2),
                              side_banks(t)(0, S, 0, 0, 1024).rearrange("p (f n) -> p f n", f=2)[:, :, 0:320]
                              .rearrange("p f (e d) -> p f e d", e=5), ACT.Copy).then_inc(*sig("vb2_ready"))
                        yield 33
                        act.wait_ge(*got("pt_psum", t, 2))
                        A(pT[:, :], side_banks(t)(0, 128, 0, 0, 1280), ACT.Copy).then_inc(*sig("pt_ready"))
                        yield 40
                        side.norm(t, 1, 1)
                    elif t.ph == 1:
                        yield 5
                        act.wait_ge(*got("ca_psum", t, 1))
                        A(q_small[:, :, :, :], side_banks(t)(0, HF, 1, 0, 256).rearrange(two, a=2, b=2), ACT.Copy)\
                            .then_inc(*sig("q_ready"))
                        yield 8
                        side.exps(t, 0, smv[:, 0:8, 0:T])
                        yield 11
                        act.wait_ge(*got("pt_psum", t, 1))
                        A(pT[:, 0:512], side_banks(t)(0, 128, 2, 0, 512), ACT.Copy).then_inc(*sig("pt_ready"))
                        yield 15
                        act.wait_ge(*got("ot_psum", t, 1))
                        A(xT[:, :, :, :], side_banks(t)(0, HF, 0, 0, 256).rearrange(two, a=2, b=2), ACT.Copy)\
                            .then_inc(*sig("ot_ready"))
                        yield 17
                        act.wait_ge(*got("ca_psum", t, 2))
                        A(q_small[:, :, :, :], side_banks(t)(0, HF, 1, 0, 256).rearrange(two, a=2, b=2), ACT.Copy)\
                            .then_inc(*sig("q_ready"))
                        yield 20
                        side.exps(t, 1, p2[:, :])
                        yield 23
                        act.wait_ge(*got("pt_psum", t, 2))
                        A(pT[0:32, 0:128], side_banks(t)(0, 32, 0, 0, 128), ACT.Copy).then_inc(*sig("pt_ready"))
                        yield 27
                        act.wait_ge(*got("ot_psum", t, 2))
                        A(xT[:, :, :, :], side_banks(t)(0, HF, 0, 0, 256).rearrange(two, a=2, b=2), ACT.Copy)\
                            .then_inc(*sig("ot_ready"))
                    else:
                        yield 3
                        side.norm(t, 0, 0)
                        yield 5
                        act.wait_ge(*got("qkv_psum", t, 1))
                        A(q_small[:, :, :, :], side_banks(t)(0, HF, 1, 0, 256).rearrange(two, a=2, b=2), ACT.Copy)\
                            .then_inc(*sig("q_ready"))
                        yield 9
                        side.exps(t, 0, smv[:, :, 0:T])
                        yield 12
                        act.wait_ge(*got("pt_psum", t, 1))
                        A(pT[:, :], side_banks(t)(0, 128, 0, 0, 1280), ACT.Copy).then_inc(*sig("pt_ready"))
                        yield 16
                        act.wait_ge(*got("ot_psum", t, 1))
                        A(xT[:, :, :, :], side_banks(t)(0, HF, 1, 0, 256).rearrange(two, a=2, b=2), ACT.Copy)\
                            .then_inc(*sig("ot_ready"))
                        yield 20
                        side.norm(t, 1, 0)

                @staticmethod
                def queries(t, b):
                    for g, (h0, n) in enumerate(t.groups):
                        yield 1 + g
                        if g == 0:
                            act.wait_ge(*got("pv_done", t, per("pv_done", t) // 2 * (b - 1)))
                        act.wait_ge(*got("qt_psum", t, len(t.groups) * b + g + 1))
                        q = slice(T * h0, T * (h0 + n))
                        A(q_hi[0:DC, b, q].rearrange("p (h s) -> p h s", h=n),
                          C(0, DC, g, 0, S * n).rearrange("p (h s) -> p h s", h=n)[:, :, 0:T], ACT.Copy)\
                            .then_inc(*sig("qh_ready"))

                @staticmethod
                def context(t, b):
                    for r in range(NPIECE):
                        yield 1 + r
                        act.wait_ge(*got("ct_psum", t, NPIECE * b + r + 1))
                        A(ctxT_hi[0:DC, b, PIECE * r:PIECE * r + PIECE], C(0, DC, r % banks(t), 0, PIECE), ACT.Copy)\
                            .then_inc(*sig("cth_ready"))

                @staticmethod
                def maxima(t, b):
                    yield 3 * t.heads // 2 + 4
                    act.wait_ge(*got("mr_psum", t, b + 1))
                    for g, (h0, n) in enumerate(t.groups):
                        z = A(q_hi[DC:DC + 1, b, T * h0:T * (h0 + n)], C(DC, 1, g, 0, T * n), ACT.Copy, scale=-1.0)
                    z.then_inc(*sig("mr_ready"))

                @staticmethod
                def post(t, last=False):
                    if t.ph == 1:
                        return
                    yield 7
                    act.wait_ge(*got("xnf_psum", t, 1))
                    for i in range(2):
                        z = A(hF[:, i, :, :], C(0, HF, 1, 128 * i, 128).rearrange("p (b s) -> p b s", b=2),
                              ACT.Identity, scale=gb[:, i, 4:5], bias=gb[:, i, 5:6])
                    z.then_inc(*sig("hf_ready"))
                    yield 10
                    act.wait_ge(*got("f_psum", t, 1))
                    for c in range(5):
                        z = A(gT[:, c, :], FC(5 + c), ACT.Gelu_apprx_tanh if t.ph == 0 else ACT.Gelu,
                              bias=bff[:, 5 + c:6 + c])
                    z.then_inc(*sig("gelu_ready"))

            def main(t, b, first=False, last=False):
                G = t.groups
                total = NC * len(G)

                def copy_out(b, some):
                    for g in some:
                        h0, nh = G[g]
                        if g == 0:
                            act.wait_ge(*got("ut_ready", t, b))
                        act.wait_ge(*got("pv_done", t, total * b + total - len(G) + g + 1))
                        A(u_sb[:, T * h0:T * (h0 + nh)], ps_u[0:DC + 1, g, 0:T * nh], ACT.Copy)\
                            .then_inc(*sig("u_copied"))

                for n in range(total):
                    yield 2 * n + 1
                    c, g = divmod(n, len(G))
                    kp = KP if c < 8 or t.ph != 1 else KP - 1
                    w, k = T * G[g][1], total * b + n
                    act.wait_ge(*got("sc_psum", t, k + 1))
                    act.wait_ge(*got("pl_ready", t, k - 1))
                    A(p32[0:kp, k % 2, 0:w], ps_s[0:kp, k % 2, 0:w], ACT.Exp, scale=DH[t.ph] ** -0.5)
                    act.wait_ge(*got("pv_done", t, k - 2))
                    A(p_hi[0:kp, k % 3, 0:w], ps_s[0:kp, k % 2, 0:w], ACT.Exp, scale=DH[t.ph] ** -0.5)\
                        .then_inc(*sig("exp_done"))
                    if n < 2 and not first:
                        yield 2 * n + 2
                        copy_out(b - 1, range(len(G) - 1, len(G)) if n else range(len(G) - 1))
                if last:
                    yield 2 * total + 2
                    copy_out(b, range(len(G)))

            schedule(act, side, main)

        wrong = {}
        for name, s in sg.items():
            if name.endswith(("_loaded", "_saved")):
                continue
            seen = tuple(s.seen.get(ph, 0) for ph in range(3))
            if seen != s.counts:
                wrong[name] = (seen, s.counts)
        assert not wrong, wrong


def kernel(**inputs):
    import concourse.bacc as bacc
    from concourse.bass_utils import run_bass_kernel_spmd

    nc = bacc.Bacc("TRN2", target_bir_lowering=False, num_devices=1)
    arrays, args = {}, {}

    def give(name, v):
        v = np.ascontiguousarray(v)
        arrays[f"in_{name}"] = v
        return nc.dram_tensor(f"in_{name}", v.shape, mybir.dt.from_np(v.dtype), kind="ExternalInput").ap()

    for name, v in inputs.items():
        args[name] = give(name, v)
    sel = np.zeros((DC, S), np.float32)
    chosen = np.linspace(0, DC - 1, T).astype(np.int64)
    sel[chosen, np.arange(T)] = 1.0
    f = np.arange(HF)
    hmask = np.concatenate([f[:, None] // 20 == np.arange(4), f[:, None] // 8 == np.arange(10)], 1)
    hmask32 = np.arange(32)[:, None] // NCA == np.arange(D) // 20
    consts = [give(n, v.astype(np.float32)) for n, v in (("sel", sel), ("hmask", hmask), ("hmask32", hmask32))]
    out = nc.dram_tensor("out", (B, T, D), F32, kind="ExternalOutput").ap()
    xattn_stack(nc, args, *consts, out)
    r = run_bass_kernel_spmd(nc, [arrays], core_ids=[0])
    return r.results[0]["out"]
```
